# Optimizing a Trainium2 kernel written in Bass

```python
import numpy as np
import jax
import jax.numpy as jnp

def _softmax(x, axis=-1):
    return jax.nn.softmax(x, axis=axis)

def _gelu(x):
    return jax.nn.gelu(x, approximate=True)

def _silu(x):
    return jax.nn.silu(x)

def _sigmoid(x):
    return jax.nn.sigmoid(x)

def _layernorm(x, axis=-1, eps=1e-05):
    m = jnp.mean(x, axis=axis, keepdims=True)
    v = jnp.var(x, axis=axis, keepdims=True)
    return (x - m) / jnp.sqrt(v + eps)

def _scatter_add(tgt, idx, src, axis=0):
    return tgt.at[idx].add(src)

def _segment_sum(src, seg, n):
    return jax.ops.segment_sum(src, seg, n)
kernel_name = 'mk_macaron_d1_jaxref_r8_fe181d'

def setup_inputs(seed: int=0):
    np.random.seed(seed)
    _w = jnp.asarray

    def _L0_attn_setup():
        import jax, jax.numpy as jnp
        import numpy as np
        NUM_HEADS = 16
        PHI = 1.6180339887
        STRIDE = 4
        LOCAL = 8

        def _strided_allowed(S):
            i = jnp.arange(S)[:, None]
            j = jnp.arange(S)[None, :]
            return (j % STRIDE == 0) | (jnp.abs(i - j) <= LOCAL)
        key = jax.random.key(seed)
        ks = jax.random.split(key, 6)
        B, S, H = (2, 256, 128)
        scale = H ** (-0.5)
        x = jax.random.normal(ks[0], (B, S, H), jnp.float32)
        q_w = jax.random.normal(ks[1], (H, H), jnp.float32) * scale
        k_w = jax.random.normal(ks[2], (H, H), jnp.float32) * scale
        v_w = jax.random.normal(ks[3], (H, H), jnp.float32) * scale
        o_w = jax.random.normal(ks[4], (H, H), jnp.float32) * scale
        o_b = jax.random.normal(ks[5], (H,), jnp.float32) * 0.01
        unity_scale = jnp.asarray(PHI, jnp.float32)
        return {'x': x, 'q_w': q_w, 'k_w': k_w, 'v_w': v_w, 'o_w': o_w, 'o_b': o_b, 'unity_scale': unity_scale}
    _L0_attn_in = _L0_attn_setup()

    def _L0_ffn_setup():
        import jax, jax.numpy as jnp
        import numpy as np
        D_MODEL = 128
        EXPANSION = 4
        D_HIDDEN = D_MODEL * EXPANSION
        NUM_STAGES = int(np.log2(D_HIDDEN))

        def butterfly(y, weights, dim):
            lead = y.shape[:-1]
            for stage in range(weights.shape[0]):
                s = 2 ** stage
                nb = dim // (2 * s)
                yr = y.reshape(*lead, nb, 2, s)
                a = yr[..., 0, :]
                b = yr[..., 1, :]
                w = weights[stage].reshape(nb, s, 2, 2)
                na = w[..., 0, 0] * a + w[..., 0, 1] * b
                nb2 = w[..., 1, 0] * a + w[..., 1, 1] * b
                y = jnp.stack([na, nb2], axis=-2).reshape(*lead, dim)
            return y
        key = jax.random.key(seed)
        ks = jax.random.split(key, 6)
        B, S = (4, 256)
        x = jax.random.normal(ks[0], (B, S, D_MODEL), jnp.float32)
        W_exp = jax.random.normal(ks[1], (D_MODEL, D_HIDDEN), jnp.float32) * 0.02
        b_exp = jnp.zeros((D_HIDDEN,), jnp.float32)
        up_weights = jax.random.normal(ks[2], (NUM_STAGES, D_HIDDEN // 2, 2, 2), jnp.float32) * 0.02
        up_bias = jnp.zeros((D_HIDDEN,), jnp.float32)
        down_weights = jax.random.normal(ks[3], (NUM_STAGES, D_HIDDEN // 2, 2, 2), jnp.float32) * 0.02
        W_con = jax.random.normal(ks[4], (D_HIDDEN, D_MODEL), jnp.float32) * 0.02
        b_con = jnp.zeros((D_MODEL,), jnp.float32)
        down_bias = jnp.zeros((D_MODEL,), jnp.float32)
        return dict(x=x, W_exp=W_exp, b_exp=b_exp, up_weights=up_weights, up_bias=up_bias, down_weights=down_weights, W_con=W_con, b_con=b_con, down_bias=down_bias)
    _L0_ffn_in = _L0_ffn_setup()
    _d = {'L0_attn_x': _L0_attn_in['x'], 'L0_attn_q_w': _L0_attn_in['q_w'], 'L0_attn_k_w': _L0_attn_in['k_w'], 'L0_attn_v_w': _L0_attn_in['v_w'], 'L0_attn_o_w': _L0_attn_in['o_w'], 'L0_attn_o_b': _L0_attn_in['o_b'], 'L0_attn_unity_scale': _L0_attn_in['unity_scale'], 'L0_ffn_W_exp': _L0_ffn_in['W_exp'], 'L0_ffn_b_exp': _L0_ffn_in['b_exp'], 'L0_ffn_up_weights': _L0_ffn_in['up_weights'], 'L0_ffn_up_bias': _L0_ffn_in['up_bias'], 'L0_ffn_down_weights': _L0_ffn_in['down_weights'], 'L0_ffn_W_con': _L0_ffn_in['W_con'], 'L0_ffn_b_con': _L0_ffn_in['b_con'], 'L0_ffn_down_bias': _L0_ffn_in['down_bias']}
    _x0 = _d['L0_attn_x']
    _d['L0_attn_x'] = jax.random.normal(jax.random.fold_in(jax.random.key(seed), 1), (1, 2048, 128), dtype=_x0.dtype)
    del _x0
    return _d

def reference(L0_attn_x, L0_attn_q_w, L0_attn_k_w, L0_attn_v_w, L0_attn_o_w, L0_attn_o_b, L0_attn_unity_scale, L0_ffn_W_exp, L0_ffn_b_exp, L0_ffn_up_weights, L0_ffn_up_bias, L0_ffn_down_weights, L0_ffn_W_con, L0_ffn_b_con, L0_ffn_down_bias):

    def _L0_attn_ref(x, q_w, k_w, v_w, o_w, o_b, unity_scale):
        import jax, jax.numpy as jnp
        import numpy as np
        NUM_HEADS = 16
        PHI = 1.6180339887
        STRIDE = 4
        LOCAL = 8

        def _strided_allowed(S):
            i = jnp.arange(S)[:, None]
            j = jnp.arange(S)[None, :]
            return (j % STRIDE == 0) | (jnp.abs(i - j) <= LOCAL)
        B, S, H = x.shape
        NH = NUM_HEADS
        D = H // NH
        q = (x @ q_w).reshape(B, S, NH, D).transpose(0, 2, 1, 3)
        k = (x @ k_w).reshape(B, S, NH, D).transpose(0, 2, 1, 3)
        v = (x @ v_w).reshape(B, S, NH, D).transpose(0, 2, 1, 3)
        q = q * jax.nn.sigmoid(unity_scale)
        scores = jnp.einsum('bhqd,bhkd->bhqk', q, k) / jnp.sqrt(jnp.asarray(D, x.dtype))
        allowed = _strided_allowed(S)
        scores = jnp.where(allowed, scores, -jnp.inf)
        attn = jax.nn.softmax(scores, axis=-1)
        out = jnp.einsum('bhqk,bhkd->bhqd', attn, v)
        out = out.transpose(0, 2, 1, 3).reshape(B, S, H)
        return out @ o_w + o_b

    def _L0_ffn_ref(x, W_exp, b_exp, up_weights, up_bias, down_weights, W_con, b_con, down_bias):
        import jax, jax.numpy as jnp
        import numpy as np
        D_MODEL = 128
        EXPANSION = 4
        D_HIDDEN = D_MODEL * EXPANSION
        NUM_STAGES = int(np.log2(D_HIDDEN))

        def butterfly(y, weights, dim):
            lead = y.shape[:-1]
            for stage in range(weights.shape[0]):
                s = 2 ** stage
                nb = dim // (2 * s)
                yr = y.reshape(*lead, nb, 2, s)
                a = yr[..., 0, :]
                b = yr[..., 1, :]
                w = weights[stage].reshape(nb, s, 2, 2)
                na = w[..., 0, 0] * a + w[..., 0, 1] * b
                nb2 = w[..., 1, 0] * a + w[..., 1, 1] * b
                y = jnp.stack([na, nb2], axis=-2).reshape(*lead, dim)
            return y
        h = jnp.einsum('bsd,dh->bsh', x, W_exp) + b_exp
        h = butterfly(h, up_weights, D_HIDDEN)
        h = jax.nn.gelu(h + up_bias, approximate=False)
        h = butterfly(h, down_weights, D_HIDDEN)
        y = jnp.einsum('bsh,hd->bsd', h, W_con) + b_con
        return y + down_bias
    x = L0_attn_x
    x = x + 0.5 * _L0_ffn_ref(_layernorm(x, axis=-1), L0_ffn_W_exp, L0_ffn_b_exp, L0_ffn_up_weights, L0_ffn_up_bias, L0_ffn_down_weights, L0_ffn_W_con, L0_ffn_b_con, L0_ffn_down_bias)
    x = x + _L0_attn_ref(_layernorm(x, axis=-1), L0_attn_q_w, L0_attn_k_w, L0_attn_v_w, L0_attn_o_w, L0_attn_o_b, L0_attn_unity_scale)
    x = x + 0.5 * _L0_ffn_ref(_layernorm(x, axis=-1), L0_ffn_W_exp, L0_ffn_b_exp, L0_ffn_up_weights, L0_ffn_up_bias, L0_ffn_down_weights, L0_ffn_W_con, L0_ffn_b_con, L0_ffn_down_bias)
    return x

_drawn_inputs = setup_inputs


def setup_inputs(seed=0):
    import zlib

    import numpy as np

    out = dict(_drawn_inputs(seed))
    spreads = {'L0_ffn_b_exp': (0.0, 0.1),
     'L0_ffn_up_bias': (0.0, 0.1),
     'L0_ffn_b_con': (0.0, 0.1),
     'L0_ffn_down_bias': (0.0, 0.1)}
    factors = {'L0_attn_o_b': 4.896}
    for name, (base, spread) in spreads.items():
        noise = np.random.default_rng([zlib.crc32(name.encode()), seed]).standard_normal(out[name].shape)
        drawn = base * np.exp(spread * noise) if base else spread * noise
        out[name] = jnp.asarray(drawn.astype(out[name].dtype))
    for name, factor in factors.items():
        out[name] = (out[name] * factor).astype(out[name].dtype)
    return out
```

```python
from contextlib import ExitStack

import numpy as np

import concourse.bass as bass
from concourse import mybir

F32 = mybir.dt.float32
BF16 = mybir.dt.bfloat16
ACT = mybir.ActivationFunctionType
ALU = mybir.AluOpType
AX = mybir.AxisListType

P = 128
S = 2048
NT = S // P
QB = 512
NB = S // QB
TB = QB // P
HID = 512
NC = HID // P
STAGES = 9
NH = 16
D = 8
G = 4
NG = NH // G
STRIDE = 4
LOCAL = 8
KEYS = S // STRIDE
NCH = KEYS // P
PARTS = 3
PROD = PARTS * PARTS * D
ROWS = PROD + PARTS
W = 64
NW = QB // W
WIN = 3 * (W + 2 * LOCAL) // 4
WSTEP = 3 * W // 4
PADK = 3 * LOCAL // 4
LK = 3 * S // 4 + 2 * PADK
BW = 3 * QB // 4 + 2 * PADK
VC = 32
BIG = -1.0e30
EPS = 1e-5
SC = 2 * QB
NSTEP = 9


def program(nc, x, q_w, k_w, v_w, o_w, o_b, unity, w_exp, b_exp, up_w, up_b, dn_w, w_con, b_con, dn_b,
            ident, identb, mask_k, mask_q, ones_s, ones_l, out):
    x_t = x[0].rearrange("(t p) f -> p t f", p=P)
    out_t = out[0].rearrange("(t p) f -> p t f", p=P)

    ctx = ExitStack()
    with ctx:
        def sb(name, shape, dt=F32):
            return ctx.enter_context(nc.sbuf_tensor(name, shape, dt))

        def sem(name):
            return ctx.enter_context(nc.semaphore(name))

        q_st = nc.dram_tensor("q_parts", [PARTS, P, S], BF16, kind="Internal").ap()
        ks_st = nc.dram_tensor("k_strided_parts", [PARTS, P, KEYS], BF16, kind="Internal").ap()
        kl_st = nc.dram_tensor("k_local_parts", [PARTS, P, LK], BF16, kind="Internal").ap()
        m_st = nc.dram_tensor("neg_max_parts_by_query", [PARTS, NB, NH * TB, P], BF16, kind="Internal").ap()
        v_st = nc.dram_tensor("v_by_key", [S + 2 * LOCAL, NH * VC], F32, kind="Internal").ap()

        X = sb("resid", [P, NT, P])
        N_MASKS = 4
        LN_A = 2 * NT + 1
        LN_N = LN_A + 1
        FOLDS = 2 * 5 * STAGES + 1
        XN = sb("xnorm", [P, TB, P])
        XT = sb("xnorm_t", [P, QB])
        GH = sb("gelu_h", [P, NC, QB])
        UPW = sb("up_folded", [P, HID])
        UPT = sb("fold_tmp", [P, 2, HID])
        DNR = sb("down_rows", [P, HID])
        DNW = sb("down_folded", [P, NC, P])
        WCON = sb("w_con_sb", [P, NC, P])
        ARENA = sb("probs_all", [P, 9 * SC])
        WROW = ARENA[0:1, :]
        WBL = GH[0:NC, 0:4, :].rearrange("p c q -> p (c q)")[:, 0:(STAGES - 2) * HID // 2].rearrange(
            "p (s k) -> p s k", s=STAGES - 2)
        BB = sb("bias_blocks", [NC, 3, P])
        BR = sb("bias_row", [1, 3, HID])
        UBR = sb("up_bias_row", [1, HID])
        BUP = sb("bias_up", [P, NC])
        ONE = sb("ones", [1, P])
        YB = sb("ffn_bias", [P, 2, P])
        OBB = sb("o_bias", [P, P])
        STAT = sb("stats", [P, NT, 6])
        MV = sb("mean_var", [P, NT, 2])
        VE = sb("var_eps", [P, NT])
        SD = sb("std", [P, NT])
        RS = sb("rstd", [P, NT])
        ID = sb("ident_sb", [P, P])
        IDB = sb("identb_sb", [P, P], BF16)
        MK = sb("mask_k_sb", [P, QB], BF16)
        MQ = sb("mask_q_sb", [P, NT, WIN], BF16)
        QW = sb("q_w_sb", [P, P])
        KW = sb("k_w_sb", [P, P])
        VW = sb("v_w_sb", [P, P])
        OW = sb("o_w_sb", [P, P])
        UN = sb("unity_sb", [P, 1])
        SG = sb("sigm", [P, 4])
        QKA = sb("qk_all", [P, 2, 2 * QB])
        QK = QKA[:, 0, :]
        QKR = QKA[:, 1, :]
        WROW2 = QKA[0:1, :, :]
        QKP = sb("qk_parts", [P, PARTS, 2 * QB], BF16)
        VN = sb("v_block", [P, TB, NH, VC])
        VS = sb("v_strided", [P, NCH, NH, VC])
        ZR = sb("zeros", [LOCAL, NH * VC])
        ZB = sb("zerosb", [P, PARTS, PADK], BF16)
        KS = sb("k_strided", [ROWS, NH, KEYS], BF16)
        QS = sb("q_slots", [ROWS, NG, G, QB], BF16)
        KL = sb("k_local", [ROWS, NG, G, BW], BF16)
        VL = sb("v_local", [P, NG, NW, G, VC])
        PE_ = ARENA[:, 0:8 * SC].rearrange("p (a h c q) -> p a h c q", a=2, h=G, c=2)
        PL = ARENA[:, 8 * SC:9 * SC].rearrange("p (h w q) -> p h w q", h=G, w=NW // 2)
        OS = sb("o_sb", [P, QB])
        RD = sb("rden", [P, TB, G])
        CT = sb("ctx_rows", [P, TB, P])
        CTT = sb("ctx_t", [P, QB])
        MXS = sb("max_strided", [P, NH, TB])
        MXL = sb("max_local", [P, NH, TB])
        MX = sb("neg_max", [P, NH, TB])
        MT = sb("neg_max_t", [NH * TB, P])
        MR = sb("neg_max_rest", [NH * TB, P])
        MP = sb("neg_max_parts", [NH * TB, PARTS, P], BF16)
        PS = ctx.enter_context(nc.psum_tensor("ps", [P, 8, 512], F32))

        ld_x = sem("ld_x")
        ld_w = sem("ld_w")
        ld_e = sem("ld_e")
        ld_c = sem("ld_c")
        ld_b = sem("ld_b")
        zero_set = sem("zero_set")
        pads_out = sem("pads_out")
        wbc = sem("wbc")
        fold = sem("fold")
        wct = sem("wct")
        dnt = sem("dnt")
        up_done = sem("up_done")
        dn_done = sem("dn_done")
        bias_fold = sem("bias_fold")
        bias_move = sem("bias_move")
        bias_t = sem("bias_t")
        bias_done = sem("bias_done")
        ln_step = sem("ln_step")
        ln_sd = sem("ln_sd")
        xn_ready = sem("xn_ready")
        xt_ps = sem("xt_ps")
        xt_ready = sem("xt_ready")
        h_ps = sem("h_ps")
        g_ready = sem("g_ready")
        y_ps = sem("y_ps")
        y_done = sem("y_done")
        r_ready = sem("r_ready")
        x_out = sem("x_out")
        qx_ready = sem("qx_ready")
        qt_ps = sem("qt_ps")
        qt_ready = sem("qt_ready")
        qkv_ps = sem("qkv_ps")
        qk_ready = sem("qk_ready")
        v_ready = sem("v_ready")
        split = sem("split")
        parts_out = sem("parts_out")
        v_out = sem("v_out")
        sig = sem("sig")
        ld_ks = sem("ld_ks")
        ld_mq = sem("ld_mq")
        mx_ps = sem("mx_ps")
        mx_red = sem("mx_red")
        mx_step = sem("mx_step")
        mt_ps = sem("mt_ps")
        mt_step = sem("mt_step")
        mx_out = sem("mx_out")
        ld_q = [sem(f"ld_q{g}") for g in range(NG)]
        s_ps = sem("s_ps")
        p_ready = sem("p_ready")
        pv_half = sem("pv_half")
        o_ps = sem("o_ps")
        o_sb = sem("o_sb")
        ot_ps = sem("ot_ps")
        o_den = sem("o_den")
        o_ctx = sem("o_ctx")
        ct_ps = sem("ct_ps")
        ct_sb = sem("ct_sb")
        op_ps = sem("op_ps")
        x2_done = sem("x2_done")
        one_set = sem("one_set")
        vl_zero = sem("vl_zero")
        bias_move2 = sem("bias_move2")
        r2_ready = sem("r2_ready")
        UPW2 = UPT[:, 0, :]
        DNF = UPW[:, :]

        def at(eng, per, it, k):
            return per * it + k if isinstance(it, int) else eng.snap(it * per + k)

        def tile_at(eng, it, per, k):
            return slice(per * it + k, per * it + k + 1) if isinstance(it, int) else bass.ds(eng.snap(it * per + k), 1)

        block = ctx.enter_context(nc.Block())

        @block.sync
        def _(sp):
            sp.dma_start(WROW[:, :], up_w.rearrange("s k a b -> (s k a b)")[None, :]).then_inc(ld_w, 16)
            sp.dma_start(UPW[:, :], w_exp).then_inc(ld_e, 16)
            sp.dma_start(X[:, :, :], x_t).then_inc(ld_x, 16)
            sp.dma_start(ID[:, :], ident).then_inc(ld_c, 16)
            sp.dma_start(WCON[:, :, :], w_con.rearrange("(c p) d -> p c d", p=P)).then_inc(ld_c, 16)
            sp.dma_start(QW[:, :], q_w).then_inc(ld_c, 16)
            sp.dma_start(KW[:, :], k_w).then_inc(ld_c, 16)
            sp.dma_start(VW[:, :], v_w).then_inc(ld_c, 16)
            sp.dma_start(OW[:, :], o_w).then_inc(ld_c, 16)
            sp.dma_start(UN[:, :], unity[None, :].partition_broadcast(P).rearrange("p a b -> p (a b)")).then_inc(ld_c, 16)
            sp.dma_start(YB[:, 0, :], b_con.partition_broadcast(P)).then_inc(ld_c, 16)
            sp.dma_start(YB[:, 1, :], dn_b.partition_broadcast(P)).then_inc(ld_c, 16)
            sp.dma_start(OBB[:, :], o_b.partition_broadcast(P)).then_inc(ld_c, 16)
            sp.dma_start(IDB[:, :], identb).then_inc(ld_c, 16)
            sp.dma_start(MK[:, :], mask_k).then_inc(ld_c, 16)
            sp.dma_start(MQ[:, :, :], mask_q).then_inc(ld_c, 16)
            sp.wait_ge(zero_set, N_MASKS)
            for a in (0, LK - PADK):
                sp.dma_start(kl_st[:, :, a:a + PADK].rearrange("i p k -> p i k"), ZB[:, :, :]).then_inc(pads_out, 16)
            for a in (0, S + LOCAL):
                sp.dma_start(v_st[a:a + LOCAL, :], ZR[:, :]).then_inc(pads_out, 16)
            sp.wait_ge(wbc, STAGES)
            sp.wait_ge(ld_w, 16)
            sp.dma_start(WROW[:, :], dn_w.rearrange("s k a b -> (s k a b)")[None, :]).then_inc(ld_w, 16)
            for b in range(NB):
                sp.wait_ge(split, 4 * b + 4)
                sp.dma_start(q_st[:, :, b * QB:(b + 1) * QB].rearrange("i p s -> p i s"),
                             QKP[:, :, 0:QB]).then_inc(parts_out, 16)
                sp.dma_start(ks_st[:, :, b * P:(b + 1) * P].rearrange("i p s -> p i s"),
                             QKP[:, :, QB:QB + P]).then_inc(parts_out, 16)
                sp.dma_start(kl_st[:, :, PADK + 3 * P * b:PADK + 3 * P * (b + 1)].rearrange("i p s -> p i s"),
                             QKP[:, :, QB + P:2 * QB]).then_inc(parts_out, 16)
                sp.wait_ge(v_ready, 2 * b + 1)
                sp.dma_start(v_st[LOCAL + b * QB:LOCAL + (b + 1) * QB, :].rearrange("(t p) c -> p t c", p=P),
                             VN[:, :, :, :].rearrange("p t h c -> p t (h c)")).then_inc(v_out, 16)
            sp.wait_ge(parts_out, 16 * 3 * NB)
            sp.wait_ge(pads_out, 16 * 4)
            sp.wait_ge(v_out, 16 * NB)
            for i in range(PARTS):
                for j in range(PARTS):
                    r = (i * PARTS + j) * D
                    sp.dma_start(KS[r:r + D, :, :], ks_st[j].rearrange("(h d) k -> d h k", d=D)).then_inc(ld_ks, 16)
            sp.dma_start(KS[PROD:ROWS, :, :], ones_s).then_inc(ld_ks, 16)

            def load_slot(it, g, done):
                hs = slice(G * D * g, G * D * (g + 1))
                for i in range(PARTS):
                    for j in range(PARTS):
                        r = (i * PARTS + j) * D
                        sp.dma_start(QS[r:r + D, g, :, :], q_st[i, hs, it * QB:(it + 1) * QB].rearrange(
                            "(h d) s -> d h s", d=D)).then_inc(done, 16)
                        sp.dma_start(KL[r:r + D, g, :, :], kl_st[j, hs, it * 3 * P:it * 3 * P + BW].rearrange(
                            "(h d) k -> d h k", d=D)).then_inc(done, 16)

            for it in range(NB):
                if it:
                    sp.wait_ge(mx_ps, 5 * TB * it)
                for g in range(NG):
                    load_slot(it, g, ld_mq)
                sp.wait_ge(mt_step, 5 * it + 5)
                sp.dma_start(m_st[:, it].rearrange("i r c -> r i c"), MP[:, :, :]).then_inc(mx_out, 16)
            sp.wait_ge(mx_out, 16 * NB)
            sp.wait_ge(vl_zero, 1)

            for it in range(NB):
                for g in range(NG):
                    if it == 0:
                        sp.wait_ge(mx_ps, 5 * TB * NB)
                    else:
                        sp.wait_ge(o_ps, NG * (it - 1) + g + 1)
                    load_slot(it, g, ld_q[g])
                    hs = slice(G * g, G * g + G)
                    sp.dma_start(QS[PROD:ROWS, g, :, :],
                                 m_st[:, it, G * g * TB:(G * g + G) * TB, :].rearrange("i (h t) c -> i h (t c)", h=G)
                                 ).then_inc(ld_q[g], 16)
                    sp.dma_start(KL[PROD:ROWS, g, :, :], ones_l[:, hs, it * 3 * P:it * 3 * P + BW]).then_inc(ld_q[g], 16)
                    for w in range(NW):
                        k0 = it * QB + w * W
                        src = v_st[k0:k0 + W + 2 * LOCAL, G * g * VC:(G * g + G) * VC].rearrange(
                            "(a r) c -> a r c", r=STRIDE)[:, 1:STRIDE, :]
                        p0 = W * (w % 2)
                        sp.dma_start(VL[p0:p0 + WIN, g, w, :, :].rearrange("p h c -> p (h c)"), src).then_inc(ld_q[g], 16)
            for b in range(NB):
                sp.wait_ge(y_done, NB + b + 1)
                sp.dma_start(out_t[:, b * TB:(b + 1) * TB, :], X[:, b * TB:(b + 1) * TB, :]).then_inc(x_out, 16)
            sp.wait_ge(x_out, 16 * NB)

        @block.gpsimd
        def _(pool):
            for st in range(STAGES - 2):
                pool.dma_start(WBL[:, st, :], up_w[st].rearrange("(c k) a b -> c (k a b)", c=NC)).then_inc(ld_b, 16)
            pool.dma_start(WROW2, up_w[STAGES - 2:STAGES].rearrange("s k a b -> s (k a b)")[None, :, :]).then_inc(ld_b, 16)
            pool.dma_start(BB[:, 0, :], b_exp.rearrange("(c p) -> c p", c=NC)).then_inc(ld_b, 16)
            pool.dma_start(UBR[:, :], up_b[None, :]).then_inc(ld_b, 16)
            pool.memset(ZR[:, :], 0.0).then_inc(zero_set, 1)
            pool.memset(ZB[:, :, :], 0.0).then_inc(zero_set, 1)
            pool.memset(VN[:, :, :, :], 0.0).then_inc(bias_fold, 1)
            pool.memset(VS[:, :, :, :], 0.0).then_inc(bias_fold, 1)
            pool.wait_ge(bias_fold, 2)
            pool.memset(VN[:, :, :, D:D + 1], 1.0).then_inc(zero_set, 1)
            pool.memset(VS[:, :, :, D:D + 1], 1.0).then_inc(zero_set, 1)
            k = 2

            def stage(w4, y, z, t, s, parts):
                nonlocal k
                n = y.shape[1] // (2 * s)
                yv = y.rearrange("p (n i s) -> p n i s", n=n, i=2)
                zv = z.rearrange("p (n i s) -> p n i s", n=n, i=2)
                tv = t.rearrange("p (n i s) -> p n i s", n=n, i=2)
                wv = w4.rearrange("p (n s) c -> p n c s", n=n)
                for o in range(2):
                    pool.tensor_tensor(zv[:, :, o, :], yv[:, :, o, :], wv[:, :, 3 * o, :], ALU.mult).then_inc(bias_fold, 1)
                    pool.tensor_tensor(tv[:, :, o, :], yv[:, :, 1 - o, :], wv[:, :, 1 + o, :], ALU.mult).then_inc(bias_fold, 1)
                k += 4
                pool.wait_ge(bias_fold, k)
                pool.tensor_tensor(z, z, t, ALU.add).then_inc(bias_fold, 1)
                k += 1
                pool.wait_ge(bias_fold, k)

            pool.wait_ge(ld_b, 16 * (STAGES + 1))
            a, b = 0, 1
            for st in range(STAGES - 2):
                stage(WBL[:, st, :].rearrange("p (k c) -> p k c", c=4), BB[:, a, :], BB[:, b, :], BB[:, 2, :], 2 ** st, NC)
                a, b = b, a
            for c in range(NC):
                pool.dma_start(BR[:, 0, c * P:(c + 1) * P], BB[c:c + 1, a, :]).then_inc(bias_move, 16)
            pool.wait_ge(bias_move, 16 * NC)
            a, b = 0, 1
            for st in range(STAGES - 2, STAGES):
                stage(WROW2[:, st - STAGES + 2, :].rearrange("p (k c) -> p k c", c=4), BR[:, a, :], BR[:, b, :], BR[:, 2, :], 2 ** st, 1)
                a, b = b, a
            assert a == 0
            pool.tensor_tensor(BR[:, 1, :], BR[:, 0, :], UBR[:, :], ALU.add).then_inc(bias_done, 1)

        @block.tensor
        def _(pe):
            pe.wait_ge(zero_set, N_MASKS)
            pe.wait_ge(one_set, 1)
            for f in range(2):
                pe.wait_ge(ld_w, 16 * (f + 1))
                for i in range(STAGES):
                    st = i if f == 0 else STAGES - 1 - i
                    n = f * STAGES + i
                    if n >= 2:
                        pe.wait_ge(fold, 5 * (n - 1) + (n - 2 >= STAGES))
                    for c in range(2):
                        o = st * 2 * HID + c * HID
                        mm = pe.matmul(PS[:, 2 * (n % 2) + c, :], ONE[:, :], WROW[:, o:o + HID], start=True, stop=True)
                    mm.then_inc(wbc, 1)
                if f == 0:
                    pe.wait_ge(ld_c, 16 * 13)
                    for c in range(NC):
                        mm = pe.transpose(PS[:, 4, c * P:(c + 1) * P], WCON[:, c, :], ID[:, :])
                    mm.then_inc(wct, 1)
            pe.wait_ge(bias_done, 1)
            for c in range(NC):
                mm = pe.matmul(PS[:, 5, c:c + 1], BR[:, 1, c * P:(c + 1) * P], ONE[:, 0:1], start=True, stop=True)
            mm.then_inc(bias_t, 1)
            pe.wait_ge(fold, FOLDS)
            for c in range(NC):
                mm = pe.transpose(PS[:, 6, c * P:(c + 1) * P], DNF[:, c * P:(c + 1) * P], ID[:, :])
            mm.then_inc(dnt, 1)

            def transpose_block(b):
                pe.wait_ge(xn_ready, b + 1)
                if b == 0:
                    pe.wait_ge(dn_done, 1)
                    pe.wait_ge(bias_move2, 1)
                else:
                    pe.wait_ge(xt_ready, b)
                for t in range(TB):
                    mm = pe.transpose(PS[:, 0, t * P:(t + 1) * P], XN[:, t, :], ID[:, :])
                mm.then_inc(xt_ps, 1)

            def ffn(b, ahead):
                pe.wait_ge(xt_ready, b + 1)
                for c in range(NC):
                    if b % NB:
                        pe.wait_ge(g_ready, NC * (b - 1) + c + 1)
                    pe.matmul(PS[:, 1 + c, :], UPW2[:, c * P:(c + 1) * P], XT[:, :], start=True, stop=True).then_inc(h_ps, 1)
                if ahead:
                    transpose_block(b + 1)
                pe.wait_ge(g_ready, NC * (b + 1))
                if b % NB:
                    pe.wait_ge(y_done, b)
                for t in range(TB):
                    for c in range(NC):
                        mm = pe.matmul(PS[:, 5, t * P:(t + 1) * P], GH[:, c, t * P:(t + 1) * P], DNW[:, c, :],
                                       start=(c == 0), stop=(c == NC - 1))
                mm.then_inc(y_ps, 1)

            transpose_block(0)
            for b in range(NB):
                ffn(b, b < NB - 1)

            for b in range(NB):
                pe.wait_ge(qx_ready, b + 1)
                if b == 0:
                    pe.wait_ge(y_done, NB)
                else:
                    pe.wait_ge(qt_ready, b)
                for t in range(TB):
                    mm = pe.transpose(PS[:, 0, t * P:(t + 1) * P], XN[:, t, :], ID[:, :])
                mm.then_inc(qt_ps, 1)
                pe.wait_ge(qt_ready, b + 1)
                if b:
                    pe.wait_ge(qk_ready, 2 * b)
                    pe.wait_ge(v_ready, 2 * b)
                pe.matmul(PS[:, 1, :], QW[:, :], XT[:, :], start=True, stop=True).then_inc(qkv_ps, 1)
                xs = XT[:, :].rearrange("p (a r) -> p a r", r=STRIDE)
                pe.matmul(PS[:, 2, 0:P], KW[:, :], xs[:, :, 0], start=True, stop=True)
                pe.matmul(PS[:, 2, P:QB], KW[:, :], xs[:, :, 1:STRIDE], start=True, stop=True).then_inc(qkv_ps, 1)
                for t in range(TB):
                    mm = pe.matmul(PS[:, 3, t * P:(t + 1) * P], XT[:, t * P:(t + 1) * P], VW[:, :], start=True, stop=True)
                mm.then_inc(qkv_ps, 1)
                pe.matmul(PS[:, 4, 0:P], xs[:, :, 0], VW[:, :], start=True, stop=True).then_inc(qkv_ps, 1)

            pe.wait_ge(ld_ks, 16 * 10)
            pe.wait_ge(qk_ready, 2 * NB)
            pe.wait_ge(v_ready, 2 * NB)
            for it in range(NB):
                pe.wait_ge(ld_mq, 16 * 18 * NG * (it + 1))
                for t in range(TB):
                    for j in range(NG + 1):
                        n = 5 * TB * it + 5 * t + j
                        if n >= 2:
                            pe.wait_ge(mx_red, n - 1)
                        if n == 20 * it and it:
                            pe.wait_ge(mt_step, 5 * it)
                        half = 4 * (n % 2)
                        if j < NG:
                            for h in range(G):
                                mm = pe.matmul(PS[:, half + h, :], QS[0:PROD, j, h, t * P:(t + 1) * P],
                                               KS[0:PROD, G * j + h, :], start=True, stop=True)
                        else:
                            for c in range(2):
                                pe.matmul(PS[:, half + c, 0:8 * WIN], IDB[:, :],
                                          MQ[:, TB * it + t:TB * it + t + 1, :].to_broadcast([P, 8, WIN]),
                                          start=True, stop=False, skip_group_check=True)
                                for h in range(8):
                                    hh = 8 * c + h
                                    for w in range(2):
                                        q0 = t * P + w * W
                                        k0 = (2 * t + w) * WSTEP
                                        mm = pe.matmul(PS[w * W:(w + 1) * W, half + c, h * WIN:(h + 1) * WIN],
                                                       QS[0:PROD, hh // G, hh % G, q0:q0 + W],
                                                       KL[0:PROD, hh // G, hh % G, k0:k0 + WIN],
                                                       start=False, stop=(h == 7), skip_group_check=True)
                        mm.then_inc(mx_ps, 1)
                pe.wait_ge(mx_step, 2 * (it + 1))
                pe.transpose(PS[0:NH * TB, 0, 0:P], MX[:, :, :].rearrange("p h t -> p (h t)"), ID[:, :]).then_inc(mt_ps, 1)

            pe.wait_ge(mt_step, 5 * NB)
            pe.wait_ge(mx_red, 5 * TB * NB)

            def scores(it, g, s):
                n = NSTEP * (NG * it + g) + s
                if NSTEP * g + s >= 3:
                    pe.wait_ge(p_ready, n - 2)
                b0 = 2 * (s % 3)
                if s < 8:
                    pair, h = s // G, s % G
                    for c in range(2):
                        ch = 2 * pair + c
                        mm = pe.matmul(PS[:, b0 + c, :], KS[:, G * g + h, ch * P:(ch + 1) * P], QS[:, g, h, :],
                                       start=True, stop=True)
                else:
                    for c in range(2):
                        pe.matmul(PS[:, b0 + c, :], IDB[:, :], MK[:, :], start=True, stop=False, skip_group_check=True)
                        for i in range(2):
                            h = 2 * c + i
                            for w in range(NW):
                                p0 = W * (w % 2)
                                c0 = i * QB // 2 + (w // 2) * W
                                mm = pe.matmul(PS[p0:p0 + WIN, b0 + c, c0:c0 + W],
                                               KL[:, g, h, w * WSTEP:w * WSTEP + WIN], QS[:, g, h, w * W:(w + 1) * W],
                                               start=False, stop=(w == NW - 1), skip_group_check=True)
                mm.then_inc(s_ps, 1)

            def values(it, g, pair, c):
                n = NG * it + g
                if pair == 0 and c == 0:
                    pe.wait_ge(p_ready, NSTEP * n + 4)
                    if g:
                        pe.wait_ge(o_sb, n)
                if pair == 1 and c == 0:
                    pe.wait_ge(p_ready, NSTEP * n + 8)
                for h in range(G):
                    mm = pe.matmul(PS[VC * h:VC * (h + 1), 6, :], VS[:, 2 * pair + c, G * g + h, :], PE_[:, pair, h, c, :],
                                   start=(pair == 0 and c == 0), stop=False, skip_group_check=True)
                if c == 1:
                    mm.then_inc(pv_half, 1)

            def values_local(it, g):
                n = NG * it + g
                pe.wait_ge(p_ready, NSTEP * n + 9)
                for w in range(NW):
                    for h in range(G):
                        mm = pe.matmul(PS[VC * h:VC * (h + 1), 6, w * W:(w + 1) * W], VL[:, g, w, h, :],
                                       PL[:, h, w // 2, :], start=False, stop=True, skip_group_check=True)
                mm.then_inc(o_ps, 1)

            def turn(it, g):
                n = NG * it + g
                pe.wait_ge(o_sb, n + 1)
                if n and (g or it):
                    pe.wait_ge(o_ctx, n)
                for t in range(TB):
                    mm = pe.transpose(PS[:, 7, t * P:(t + 1) * P], OS[:, t * P:(t + 1) * P], ID[:, :])
                mm.then_inc(ot_ps, 1)

            for it in range(NB):
                for g in range(NG):
                    pe.wait_ge(ld_q[g], 16 * (20 + NW) * (it + 1))
                    for s in range(NSTEP):
                        scores(it, g, s)
                        if g and s == 1:
                            values(it, g - 1, 1, 0)
                        if g and s == 2:
                            values(it, g - 1, 1, 1)
                        if g and s == 3:
                            values_local(it, g - 1)
                        if g and s == 5:
                            turn(it, g - 1)
                        if s == 5:
                            values(it, g, 0, 0)
                        if s == 6:
                            values(it, g, 0, 1)
                values(it, NG - 1, 1, 0)
                values(it, NG - 1, 1, 1)
                values_local(it, NG - 1)
                turn(it, NG - 1)
                pe.wait_ge(o_ctx, NG * (it + 1))
                for t in range(TB):
                    mm = pe.transpose(PS[:, 7, t * P:(t + 1) * P], CT[:, t, :], ID[:, :])
                mm.then_inc(ct_ps, 1)
                pe.wait_ge(ct_sb, it + 1)
                for t in range(TB):
                    mm = pe.matmul(PS[:, 7, t * P:(t + 1) * P], CTT[:, t * P:(t + 1) * P], OW[:, :], start=True, stop=True)
                mm.then_inc(op_ps, 1)
                pe.wait_ge(x2_done, it + 1)

            transpose_block(NB)
            for b in range(NB, 2 * NB):
                ffn(b, b < 2 * NB - 1)

        @block.scalar
        def _(act):
            act.wait_ge(ld_c, 16 * 13)
            act.activation(SG[:, 0:1], UN[:, :], ACT.Exp, scale=-1.0).then_inc(sig, 1)

            def root():
                act.activation(SD[:, :], VE[:, :], ACT.Sqrt).then_inc(ln_sd, 1)

            def ffn(b):
                act.wait_ge(xt_ps, b + 1)
                if b:
                    act.wait_ge(h_ps, NC * b)
                if b == NB:
                    act.wait_ge(qkv_ps, 4 * NB)
                act.activation(XT[:, :], PS[:, 0, :], ACT.Copy).then_inc(xt_ready, 1)
                for c in range(NC):
                    act.wait_ge(h_ps, NC * b + c + 1)
                    if b and c == 0:
                        act.wait_ge(y_ps, b)
                    if b == 0 and c == 0:
                        act.wait_ge(bias_move2, 1)
                    act.activation(GH[:, c, :], PS[:, 1 + c, :], ACT.Gelu, bias=BUP[:, c:c + 1]).then_inc(g_ready, 1)

            act.wait_ge(ln_step, LN_A)
            root()
            for b in range(NB):
                ffn(b)
            act.wait_ge(ln_step, LN_N + LN_A)
            root()
            act.wait_ge(sig, 3)
            act.wait_ge(zero_set, N_MASKS)
            for b in range(NB):
                act.wait_ge(qt_ps, b + 1)
                if b:
                    act.wait_ge(qkv_ps, 4 * b)
                act.activation(XT[:, :], PS[:, 0, :], ACT.Copy).then_inc(qt_ready, 1)
                act.wait_ge(qkv_ps, 4 * b + 1)
                if b:
                    act.wait_ge(split, 4 * b)
                act.activation(QK[:, 0:QB], PS[:, 1, :], ACT.Copy, scale=SG[:, 2:3]).then_inc(qk_ready, 1)
                act.wait_ge(qkv_ps, 4 * b + 2)
                act.activation(QK[:, QB:2 * QB], PS[:, 2, :], ACT.Copy).then_inc(qk_ready, 1)
                act.wait_ge(qkv_ps, 4 * b + 3)
                if b:
                    act.wait_ge(v_out, 16 * b)
                act.activation(VN[:, :, :, 0:D], PS[:, 3, :].rearrange("p (t h d) -> p t h d", t=TB, d=D),
                               ACT.Copy).then_inc(v_ready, 1)
                act.wait_ge(qkv_ps, 4 * b + 4)
                act.activation(VS[:, b, :, 0:D], PS[:, 4, 0:P].rearrange("p (h d) -> p h d", d=D),
                               ACT.Copy).then_inc(v_ready, 1)

            for it in range(NB):
                for g in range(NG):
                    u = NG * it + g
                    for s in range(NSTEP):
                        n = NSTEP * u + s
                        act.wait_ge(s_ps, n + 1)
                        b0 = 2 * (s % 3)
                        if s < 8:
                            pair, h = s // G, s % G
                            if u and h == 0:
                                act.wait_ge(pv_half, 2 * (u - 1) + pair + 1)
                            act.activation(PE_[:, pair, h, :, :], PS[:, b0:b0 + 2, :], ACT.Exp).then_inc(p_ready, 1)
                        else:
                            if u:
                                act.wait_ge(o_ps, u)
                            act.activation(PL[:, :, :, :].rearrange("p h w q -> p (h w q)"),
                                           PS[:, b0:b0 + 2, :].rearrange("p a q -> p (a q)"), ACT.Exp).then_inc(p_ready, 1)

            act.wait_ge(ln_step, 2 * LN_N + LN_A)
            root()
            for b in range(NB, 2 * NB):
                ffn(b)

        @block.vector
        def _(dve):
            lnc = [0]

            def ln_link(ins):
                lnc[0] += 1
                ins.then_inc(ln_step, 1)

            def ln_stats():
                for t in range(NT):
                    ln_link(dve.bn_stats(STAT[:, t, :], X[:, t, :]))
                dve.wait_ge(ln_step, lnc[0])
                for t in range(NT):
                    ln_link(dve.bn_aggr(MV[:, t, :], STAT[:, t, :]))
                dve.wait_ge(ln_step, lnc[0])
                ln_link(dve.tensor_scalar(VE[:, :], MV[:, :, 1], EPS, None, ALU.add))
                assert lnc[0] % LN_N == LN_A

            def ln_inv(n):
                dve.wait_ge(ln_sd, n)
                ln_link(dve.reciprocal(RS[:, :], SD[:, :]))
                dve.wait_ge(ln_step, lnc[0])
                assert lnc[0] % LN_N == 0

            def normalize(b, done):
                for t in range(TB):
                    i = (b % NB) * TB + t
                    ins = dve.tensor_scalar(XN[:, t, :], X[:, i, :], MV[:, i, 0:1], RS[:, i:i + 1], ALU.subtract, ALU.mult)
                ins.then_inc(done, 1)

            def add_bias(b):
                ts = slice((b % NB) * TB, (b % NB) * TB + TB)
                dve.wait_ge(xn_ready, b + 1)
                bias = YB[:, 0:1, :].to_broadcast([P, TB, P])
                dve.scalar_tensor_tensor(X[:, ts, :], bias, 0.5, X[:, ts, :], ALU.mult, ALU.add).then_inc(r_ready, 1)

            dve.memset(ONE[:, :], 1.0).then_inc(one_set, 1)
            dve.memset(VL[:, :, :, :, :].rearrange("p g w h c -> p (g w h c)"), 0.0).then_inc(vl_zero, 1)
            dve.wait_ge(ld_x, 16)
            ln_stats()
            fc = [0]

            def fold_link(ins):
                fc[0] += 1
                ins.then_inc(fold, 1)

            def stage(n, st, y, z, t, down):
                s = 2 ** st
                m = HID // (2 * s)
                yv, zv, tv = (a.rearrange("p (n i s) -> p n i s", n=m, i=2) for a in (y, z, t))
                b0 = 2 * (n % 2)
                wv = PS[:, b0:b0 + 2, :].rearrange("p a b -> p (a b)").rearrange("p (n s c) -> p n c s", n=m, c=4)
                dve.wait_ge(wbc, n + 1)
                for o in range(2):
                    cross = (2 - o) if down else (1 + o)
                    fold_link(dve.tensor_tensor(zv[:, :, o, :], yv[:, :, o, :], wv[:, :, 3 * o, :], ALU.mult))
                    fold_link(dve.tensor_tensor(tv[:, :, o, :], yv[:, :, 1 - o, :], wv[:, :, cross, :], ALU.mult))
                dve.wait_ge(fold, fc[0])
                fold_link(dve.tensor_tensor(z, z, t, ALU.add))
                dve.wait_ge(fold, fc[0])

            dve.wait_ge(ld_e, 16)
            bufs = [UPW[:, :], UPT[:, 0, :]]
            for i in range(STAGES):
                stage(i, i, bufs[i % 2], bufs[(i + 1) % 2], UPT[:, 1, :], False)
            ln_inv(1)
            normalize(0, xn_ready)
            dve.wait_ge(wct, 1)
            fold_link(dve.tensor_copy(DNR[:, :], PS[:, 4, :]))
            dve.wait_ge(fold, fc[0])
            bufs = [DNR[:, :], UPW[:, :]]
            for i in range(STAGES):
                stage(STAGES + i, STAGES - 1 - i, bufs[i % 2], bufs[(i + 1) % 2], UPT[:, 1, :], True)
            assert fc[0] == FOLDS
            dve.wait_ge(bias_t, 1)
            dve.tensor_copy(BUP[:, :], PS[:, 5, 0:NC]).then_inc(bias_move2, 1)
            dve.wait_ge(dnt, 1)
            dve.tensor_copy(DNW[:, :, :].rearrange("p c d -> p (c d)"), PS[:, 6, :]).then_inc(dn_done, 1)
            dve.wait_ge(sig, 1)
            dve.tensor_scalar(SG[:, 1:2], SG[:, 0:1], float(np.sqrt(D)), float(np.sqrt(D)), ALU.mult, ALU.add).then_inc(sig, 1)
            dve.wait_ge(sig, 2)
            dve.reciprocal(SG[:, 2:3], SG[:, 1:2]).then_inc(sig, 1)
            dve.tensor_tensor(YB[:, 0, :], YB[:, 0, :], YB[:, 1, :], ALU.add).then_inc(r_ready, 1)
            dve.wait_ge(r_ready, 1)

            def ffn(b, ahead):
                add_bias(b)
                if ahead:
                    dve.wait_ge(xt_ps, b + 1)
                    normalize(b + 1, xn_ready)
                dve.wait_ge(r_ready, b + 2)
                dve.wait_ge(y_ps, b + 1)
                ts = slice((b % NB) * TB, (b % NB) * TB + TB)
                dve.scalar_tensor_tensor(X[:, ts, :], PS[:, 5, :].rearrange("p (t d) -> p t d", t=TB), 0.5, X[:, ts, :],
                                         ALU.mult, ALU.add).then_inc(y_done, 1)

            def split_block(b):
                dve.wait_ge(qk_ready, 2 * b + 2)
                if b:
                    dve.wait_ge(parts_out, 16 * 3 * b)
                dve.tensor_copy(QKP[:, 0, :], QK).then_inc(split, 1)
                dve.wait_ge(split, 4 * b + 1)
                dve.tensor_tensor(QKR, QK, QKP[:, 0, :], ALU.subtract).then_inc(split, 1)
                dve.wait_ge(split, 4 * b + 2)
                dve.tensor_copy(QKP[:, 1, :], QKR).then_inc(split, 1)
                dve.wait_ge(split, 4 * b + 3)
                dve.tensor_tensor(QKP[:, 2, :], QKR, QKP[:, 1, :], ALU.subtract).then_inc(split, 1)

            for b in range(NB):
                ffn(b, b < NB - 1)
            dve.wait_ge(y_done, NB)
            ln_stats()
            ln_inv(2)
            for b in range(NB):
                if b:
                    dve.wait_ge(qt_ps, b)
                else:
                    dve.wait_ge(xt_ps, NB)
                normalize(b, qx_ready)
                if b:
                    split_block(b - 1)
            split_block(NB - 1)

            for it in range(NB):
                for t in range(TB):
                    for j in range(NG + 1):
                        n = 5 * TB * it + 5 * t + j
                        half = 4 * (n % 2)
                        dve.wait_ge(mx_ps, n + 1)
                        if j < NG:
                            dve.tensor_reduce(MXS[:, G * j:G * j + G, t], PS[:, half:half + 4, :], AX.X, ALU.max).then_inc(mx_red, 1)
                        else:
                            dve.tensor_reduce(MXL[:, :, t].rearrange("p (c h) -> p c h", c=2),
                                              PS[:, half:half + 2, 0:8 * WIN].rearrange("p c (h k) -> p c h k", h=8),
                                              AX.X, ALU.max).then_inc(mx_red, 1)
                dve.wait_ge(mx_red, 5 * TB * (it + 1))
                dve.tensor_tensor(MX[:, :, :], MXS[:, :, :], MXL[:, :, :], ALU.max).then_inc(mx_step, 1)
                dve.wait_ge(mx_step, 2 * it + 1)
                dve.tensor_scalar(MX[:, :, :], MX[:, :, :], -1.0, None, ALU.mult).then_inc(mx_step, 1)
                dve.wait_ge(mt_ps, it + 1)
                dve.tensor_copy(MT[:, :], PS[0:NH * TB, 0, 0:P]).then_inc(mt_step, 1)
                dve.wait_ge(mt_step, 5 * it + 1)
                if it:
                    dve.wait_ge(mx_out, 16 * it)
                dve.tensor_copy(MP[:, 0, :], MT[:, :]).then_inc(mt_step, 1)
                dve.wait_ge(mt_step, 5 * it + 2)
                dve.tensor_tensor(MR[:, :], MT[:, :], MP[:, 0, :], ALU.subtract).then_inc(mt_step, 1)
                dve.wait_ge(mt_step, 5 * it + 3)
                dve.tensor_copy(MP[:, 1, :], MR[:, :]).then_inc(mt_step, 1)
                dve.wait_ge(mt_step, 5 * it + 4)
                dve.tensor_tensor(MP[:, 2, :], MR[:, :], MP[:, 1, :], ALU.subtract).then_inc(mt_step, 1)

            dve.wait_ge(qx_ready, NB)
            for it in range(NB):
                ts = slice(it * TB, it * TB + TB)
                dve.tensor_tensor(X[:, ts, :], X[:, ts, :], OBB[:, None, :].to_broadcast([P, TB, P]), ALU.add).then_inc(r2_ready, 1)
                for g in range(NG):
                    n = NG * it + g
                    dve.wait_ge(o_ps, n + 1)
                    if n:
                        dve.wait_ge(ot_ps, n)
                    dve.tensor_copy(OS[:, :], PS[:, 6, :]).then_inc(o_sb, 1)
                    dve.wait_ge(ot_ps, n + 1)
                    ov = PS[:, 7, :].rearrange("p (t h c) -> p t h c", t=TB, h=G)
                    dve.reciprocal(RD[:, :, :], ov[:, :, :, D]).then_inc(o_den, 1)
                    dve.wait_ge(o_den, n + 1)
                    if g == 0 and it:
                        dve.wait_ge(ct_ps, it)
                    dve.tensor_tensor(CT[:, :, G * D * g:G * D * (g + 1)].rearrange("p t (h d) -> p t h d", h=G),
                                      ov[:, :, :, 0:D], RD[:, :, :, None].to_broadcast([P, TB, G, D]),
                                      ALU.mult).then_inc(o_ctx, 1)
                dve.wait_ge(ct_ps, it + 1)
                dve.tensor_copy(CTT[:, :], PS[:, 7, :]).then_inc(ct_sb, 1)
                dve.wait_ge(r2_ready, it + 1)
                dve.wait_ge(op_ps, it + 1)
                dve.tensor_tensor(X[:, ts, :], PS[:, 7, :].rearrange("p (t d) -> p t d", t=TB), X[:, ts, :],
                                  ALU.add).then_inc(x2_done, 1)
            dve.wait_ge(x2_done, NB)
            ln_stats()
            ln_inv(3)
            normalize(NB, xn_ready)
            for b in range(NB, 2 * NB):
                ffn(b, b < 2 * NB - 1)


def constants():
    bf = mybir.dt.np(BF16)
    n = np.arange(WIN)
    rel = STRIDE * (n // 3) + n % 3 + 1 - LOCAL
    q = np.arange(W)
    far = np.abs(rel[:, None] - q[None, :]) > LOCAL
    mk = np.full((2, W, W), BIG, np.float32)
    mk[:, :WIN, :] = np.where(far, BIG, 0.0)
    mask_k = np.tile(mk.reshape(P, W), (1, QB // W))
    mq = np.zeros((P, NT, WIN), np.float32)
    for t in range(NT):
        for w in range(2):
            key = t * P + w * W + rel
            shut = far | (key < 0)[:, None] | (key >= S)[:, None]
            mq[w * W:(w + 1) * W, t, :] = np.where(shut, BIG, 0.0).T
    ones_l = np.ones((PARTS, NH, LK), np.float32)
    ones_l[:, :, :PADK] = 0.0
    ones_l[:, :, LK - PADK:] = 0.0
    return {
        "ident": np.eye(P, dtype=np.float32), "identb": np.eye(P).astype(bf),
        "mask_k": mask_k.astype(bf), "mask_q": mq.astype(bf),
        "ones_s": np.ones((PARTS, NH, KEYS)).astype(bf), "ones_l": ones_l.astype(bf),
    }


_INS = ["L0_attn_x", "L0_attn_q_w", "L0_attn_k_w", "L0_attn_v_w", "L0_attn_o_w", "L0_attn_o_b", "L0_attn_unity_scale",
        "L0_ffn_W_exp", "L0_ffn_b_exp", "L0_ffn_up_weights", "L0_ffn_up_bias", "L0_ffn_down_weights", "L0_ffn_W_con",
        "L0_ffn_b_con", "L0_ffn_down_bias"]


def kernel(**inputs):
    import concourse.bacc as bacc
    from concourse.bass_utils import run_bass_kernel_spmd as run

    nc = bacc.Bacc("TRN2", target_bir_lowering=False, num_devices=1)
    arrays, args = {}, []
    for name in _INS:
        a = np.ascontiguousarray(inputs[name])
        arrays[name] = a.reshape(a.shape or (1,))
    arrays.update(constants())
    for name, a in arrays.items():
        args.append(nc.dram_tensor(name, a.shape, mybir.dt.from_np(a.dtype), kind="ExternalInput").ap())
    args.append(nc.dram_tensor("out", (1, S, P), F32, kind="ExternalOutput").ap())
    program(nc, *args)
    r = run(nc, [arrays], core_ids=[0])
    return r.results[0]["out"]
```

```python
from contextlib import ExitStack

import numpy as np

import concourse.bass as bass
from concourse import mybir

F32 = mybir.dt.float32
BF16 = mybir.dt.bfloat16
ACT = mybir.ActivationFunctionType
ALU = mybir.AluOpType
AX = mybir.AxisListType

P = 128
S = 2048
NT = S // P
QB = 512
NB = S // QB
TB = QB // P
HID = 512
NC = HID // P
STAGES = 9
NH = 16
D = 8
G = 4
NG = NH // G
STRIDE = 4
LOCAL = 8
KEYS = S // STRIDE
NCH = KEYS // P
PARTS = 3
PROD = PARTS * PARTS * D
ROWS = PROD + PARTS
W = 64
NW = QB // W
WIN = 3 * (W + 2 * LOCAL) // 4
WSTEP = 3 * W // 4
PADK = 3 * LOCAL // 4
LK = 3 * S // 4 + 2 * PADK
BW = 3 * QB // 4 + 2 * PADK
VC = 32
BIG = -1.0e30
EPS = 1e-5
SAFE = 40.0
SC = 2 * QB
NSTEP = 9


def program(nc, x, q_w, k_w, v_w, o_w, o_b, unity, w_exp, b_exp, up_w, up_b, dn_w, w_con, b_con, dn_b,
            ident, identb, mask_k, mask_q, head_sel, ones_s, ones_l, zeros_q, out):
    x_t = x[0].rearrange("(t p) f -> p t f", p=P)
    out_t = out[0].rearrange("(t p) f -> p t f", p=P)

    ctx = ExitStack()
    with ctx:
        def sb(name, shape, dt=F32):
            return ctx.enter_context(nc.sbuf_tensor(name, shape, dt))

        def sem(name):
            return ctx.enter_context(nc.semaphore(name))

        q_st = nc.dram_tensor("q_parts", [PARTS, PARTS, P, S], BF16, kind="Internal").ap()
        ks_st = nc.dram_tensor("k_strided_parts", [PARTS, PARTS, P, KEYS], BF16, kind="Internal").ap()
        kl_st = nc.dram_tensor("k_local_parts", [PARTS, PARTS, P, LK], BF16, kind="Internal").ap()
        m_st = nc.dram_tensor("neg_max_by_query", [PARTS, NB, NH * TB, P], BF16, kind="Internal").ap()
        v_st = nc.dram_tensor("v_local_by_key", [LK, NH * VC], F32, kind="Internal").ap()

        X = sb("resid", [P, NT, P])
        N_MASKS = 4
        LN_A = 2 * NT + 1
        LN_N = LN_A + 1
        FOLDS = 2 * 5 * STAGES + 1
        XN = sb("xnorm", [P, TB, P])
        XT = sb("xnorm_t", [P, QB])
        GH = sb("gelu_h", [P, NC, QB])
        UPW = sb("up_folded", [P, HID])
        UPT = sb("fold_tmp", [P, 2, HID])
        DNR = sb("down_rows", [P, HID])
        DNW = sb("down_folded", [P, NC, P])
        WCON = sb("w_con_sb", [P, NC, P])
        ARENA = sb("probs_all", [P, 9 * SC])
        WROW = ARENA[0:1, :]
        WBL = GH[0:NC, 0:4, :].rearrange("p c q -> p (c q)")[:, 0:(STAGES - 2) * HID // 2].rearrange(
            "p (s k) -> p s k", s=STAGES - 2)
        BB = sb("bias_blocks", [NC, 3, P])
        BR = sb("bias_row", [1, 3, HID])
        UBR = sb("up_bias_row", [1, HID])
        BUP = sb("bias_up", [P, NC])
        ONE = sb("ones", [1, P])
        YB = sb("ffn_bias", [P, 2, P])
        OBB = sb("o_bias", [P, P])
        STAT = sb("stats", [P, NT, 6])
        MV = sb("mean_var", [P, NT, 2])
        VE = sb("var_eps", [P, NT])
        SD = sb("std", [P, NT])
        RS = sb("rstd", [P, NT])
        ID = sb("ident_sb", [P, P])
        IDB = sb("identb_sb", [P, P], BF16)
        MK = sb("mask_k_sb", [P, QB], BF16)
        MQ = sb("mask_q_sb", [P, NT, WIN], BF16)
        QW = sb("q_w_sb", [P, P])
        KW = sb("k_w_sb", [P, P])
        VW = sb("v_w_sb", [P, P])
        OW = sb("o_w_sb", [P, P])
        UN = sb("unity_sb", [P, 1])
        SG = sb("sigm", [P, 4])
        WROW2 = sb("weight_rows_last", [1, 2, 2 * HID])
        QK = [ARENA[:, o:o + 4 * QB] for o in (0, 4 * QB)]
        QKR = ARENA[:, 8 * QB:12 * QB]
        QKP = ARENA[:, 12 * QB:18 * QB].bitcast(BF16).rearrange("p (i s) -> p i s", i=PARTS)
        QOF, SOF, LOF = 0, 2 * QB, 2 * QB + 2 * P
        VN = sb("v_block", [P, 3, NH, VC])
        VS = sb("v_strided", [P, NCH, NH, VC])
        ZR = sb("zeros", [PADK, NH * VC])
        ZB = sb("zerosb", [P, PADK], BF16)
        XTR = sb("xnorm_t_by_key", [P, QB])
        SQ = sb("squares", [P, 2 * QB], BF16)
        HS = sb("head_sel_sb", [P, NH], BF16)
        NM = sb("norms", [NH, NB, 2])
        NX = sb("norms_max", [NH, 4])
        FLT = sb("bound_row", [1, 4])
        FLAG = sb("bounded", [1, 1], mybir.dt.int32)
        KS = sb("k_strided", [ROWS, NH, KEYS], BF16)
        QS = sb("q_slots", [ROWS, NG, G, QB], BF16)
        KL = sb("k_local", [ROWS, NG, G, BW], BF16)
        VL = sb("v_local", [P, NG, NW, G, VC])
        PE_ = ARENA[:, 0:8 * SC].rearrange("p (a h c q) -> p a h c q", a=2, h=G, c=2)
        PL = ARENA[:, 8 * SC:9 * SC].rearrange("p (h w q) -> p h w q", h=G, w=NW // 2)
        OS = sb("o_sb", [P, QB])
        RD = sb("rden", [P, TB, G])
        CT = sb("ctx_rows", [P, TB, P])
        CTT = sb("ctx_t", [P, QB])
        MXS = sb("max_strided", [P, NH, TB])
        MXL = sb("max_local", [P, NH, TB])
        MX = sb("neg_max", [P, NH, TB])
        MT = sb("neg_max_t", [NH * TB, P])
        MR = sb("neg_max_rest", [NH * TB, P])
        MP = sb("neg_max_parts", [NH * TB, PARTS, P], BF16)
        PS = ctx.enter_context(nc.psum_tensor("ps", [P, 8, 512], F32))

        ld_x = sem("ld_x")
        ld_w = sem("ld_w")
        ld_e = sem("ld_e")
        ld_c = sem("ld_c")
        ld_b = sem("ld_b")
        zero_set = sem("zero_set")
        pads_out = sem("pads_out")
        wbc = sem("wbc")
        fold = sem("fold")
        wct = sem("wct")
        dnt = sem("dnt")
        up_done = sem("up_done")
        dn_done = sem("dn_done")
        bias_fold = sem("bias_fold")
        bias_move = sem("bias_move")
        bias_t = sem("bias_t")
        bias_done = sem("bias_done")
        ln_step = sem("ln_step")
        ln_sd = sem("ln_sd")
        xn_ready = sem("xn_ready")
        xt_ps = sem("xt_ps")
        xt_ready = sem("xt_ready")
        h_ps = sem("h_ps")
        g_ready = sem("g_ready")
        y_ps = sem("y_ps")
        y_done = sem("y_done")
        r_ready = sem("r_ready")
        x_out = sem("x_out")
        qx_ready = sem("qx_ready")
        qt_ps = sem("qt_ps")
        qt_ready = sem("qt_ready")
        qkv_ps = sem("qkv_ps")
        qk_ready = sem("qk_ready")
        v_ready = sem("v_ready")
        split = sem("split")
        parts_out = sem("parts_out")
        v_out = sem("v_out")
        sig = sem("sig")
        ld_ks = sem("ld_ks")
        ld_mq = sem("ld_mq")
        sq_done = sem("sq_done")
        nm_ps = sem("nm_ps")
        nm_step = sem("nm_step")
        bt_ps = sem("bt_ps")
        flag_set = sem("flag_set")
        mx_ps = sem("mx_ps")
        mx_red = sem("mx_red")
        mx_step = sem("mx_step")
        mt_ps = sem("mt_ps")
        mt_step = sem("mt_step")
        mx_out = sem("mx_out")
        ld_q = [sem(f"ld_q{g}") for g in range(NG)]
        s_ps = sem("s_ps")
        p_ready = sem("p_ready")
        pv_half = sem("pv_half")
        o_ps = sem("o_ps")
        o_sb = sem("o_sb")
        ot_ps = sem("ot_ps")
        o_den = sem("o_den")
        o_ctx = sem("o_ctx")
        ct_ps = sem("ct_ps")
        ct_sb = sem("ct_sb")
        op_ps = sem("op_ps")
        x2_done = sem("x2_done")
        one_set = sem("one_set")
        qtr_part = sem("qtr_part")
        qtr_ready = sem("qtr_ready")
        vl_zero = sem("vl_zero")
        bias_move2 = sem("bias_move2")
        r2_ready = sem("r2_ready")
        UPW2 = UPT[:, 0, :]
        DNF = UPW[:, :]

        def at(eng, per, it, k):
            return per * it + k if isinstance(it, int) else eng.snap(it * per + k)

        def head_rows(t, h, a, n):
            return t[:, :, D * h:D * (h + 1), a:a + n].rearrange("i j d s -> (i j) d s")

        def tripled(ap):
            return ap[:, None, :].to_broadcast([P, PARTS, ap.shape[1]])

        block = ctx.enter_context(nc.Block())

        @block.sync
        def _(sp):
            sp.dma_start(WROW[:, :], up_w.rearrange("s k a b -> (s k a b)")[None, :]).then_inc(ld_w, 16)
            sp.dma_start(UPW[:, :], w_exp).then_inc(ld_e, 16)
            sp.dma_start(X[:, :, :], x_t).then_inc(ld_x, 16)
            sp.dma_start(ID[:, :], ident).then_inc(ld_c, 16)
            sp.dma_start(WCON[:, :, :], w_con.rearrange("(c p) d -> p c d", p=P)).then_inc(ld_c, 16)
            sp.dma_start(QW[:, :], q_w).then_inc(ld_c, 16)
            sp.dma_start(KW[:, :], k_w).then_inc(ld_c, 16)
            sp.dma_start(VW[:, :], v_w).then_inc(ld_c, 16)
            sp.dma_start(OW[:, :], o_w).then_inc(ld_c, 16)
            sp.dma_start(UN[:, :], unity[None, :].partition_broadcast(P).rearrange("p a b -> p (a b)")).then_inc(ld_c, 16)
            sp.dma_start(YB[:, 0, :], b_con.partition_broadcast(P)).then_inc(ld_c, 16)
            sp.dma_start(YB[:, 1, :], dn_b.partition_broadcast(P)).then_inc(ld_c, 16)
            sp.dma_start(OBB[:, :], o_b.partition_broadcast(P)).then_inc(ld_c, 16)
            sp.dma_start(IDB[:, :], identb).then_inc(ld_c, 16)
            sp.dma_start(MK[:, :], mask_k).then_inc(ld_c, 16)
            sp.dma_start(MQ[:, :, :], mask_q).then_inc(ld_c, 16)
            sp.dma_start(HS[:, :], head_sel).then_inc(ld_c, 16)
            sp.dma_start(m_st, zeros_q).then_inc(pads_out, 16)
            sp.dma_start(KS[PROD:ROWS, :, :], ones_s).then_inc(pads_out, 16)
            sp.wait_ge(zero_set, N_MASKS)
            for a in (0, LK - PADK):
                sp.dma_start(kl_st[:, :, :, a:a + PADK].rearrange("i j p k -> p (i j) k"),
                             ZB[:, None, :].to_broadcast([P, PARTS * PARTS, PADK])).then_inc(pads_out, 16)
                sp.dma_start(v_st[a:a + PADK, :], ZR[:, :]).then_inc(pads_out, 16)
            sp.wait_ge(wbc, STAGES)
            sp.wait_ge(ld_w, 16)
            sp.dma_start(WROW[:, :], dn_w.rearrange("s k a b -> (s k a b)")[None, :]).then_inc(ld_w, 16)
            for b in range(NB):
                sp.wait_ge(v_ready, 2 * b + 1)
                sp.dma_start(v_st[PADK + 3 * P * b:PADK + 3 * P * (b + 1), :].rearrange("(t p) c -> p t c", p=P),
                             VN[:, :, :, :].rearrange("p t h c -> p t (h c)")).then_inc(v_out, 16)
                if b % 2:
                    f = b // 2
                    sp.wait_ge(split, 4 * f + 4)
                    for j in range(PARTS):
                        sp.dma_start(ks_st[:, j, :, 2 * P * f:2 * P * (f + 1)].rearrange("i p k -> p i k"),
                                     tripled(QKP[:, j, SOF:LOF])).then_inc(parts_out, 16)
                        sp.dma_start(kl_st[:, j, :, PADK + 6 * P * f:PADK + 6 * P * (f + 1)].rearrange("i p k -> p i k"),
                                     tripled(QKP[:, j, LOF:4 * QB])).then_inc(parts_out, 16)
                    for i in range(PARTS):
                        sp.dma_start(q_st[i, :, :, 2 * QB * f:2 * QB * (f + 1)].rearrange("j p s -> p j s"),
                                     tripled(QKP[:, i, QOF:SOF])).then_inc(parts_out, 16)
            sp.wait_ge(parts_out, 16 * 9 * NB // 2)
            sp.wait_ge(pads_out, 16 * 6)
            for h in range(NH):
                sp.dma_start(KS[0:PROD, h, :], head_rows(ks_st, h, 0, KEYS)).then_inc(ld_ks, 16)
            sp.wait_ge(v_out, 16 * NB)

            def load_slot(it, g, done):
                for h in range(G):
                    sp.dma_start(QS[0:PROD, g, h, :], head_rows(q_st, G * g + h, it * QB, QB)).then_inc(done, 16)
                    sp.dma_start(KL[0:PROD, g, h, :], head_rows(kl_st, G * g + h, it * 3 * P, BW)).then_inc(done, 16)

            sp.wait_ge(flag_set, 1)
            with sp.If(sp.value_load(FLAG[0:1, 0:1], min_val=0, max_val=1) == 0):
                for it in range(NB):
                    if it:
                        sp.wait_ge(mx_ps, 5 * TB * it)
                    for g in range(NG):
                        load_slot(it, g, ld_mq)
                    sp.wait_ge(mt_step, 5 * it + 5)
                    sp.dma_start(m_st[:, it].rearrange("i r c -> r i c"), MP[:, :, :]).then_inc(mx_out, 16)
                sp.wait_ge(mx_out, 16 * NB)
                sp.wait_ge(mx_ps, 5 * TB * NB)
            sp.end_ifs()
            sp.wait_ge(vl_zero, 1)

            for it in range(NB):
                for g in range(NG):
                    if it:
                        sp.wait_ge(o_ps, NG * (it - 1) + g + 1)
                    hs = slice(G * g, G * g + G)
                    load_slot(it, g, ld_q[g])
                    sp.dma_start(QS[PROD:ROWS, g, :, :],
                                 m_st[:, it, G * g * TB:(G * g + G) * TB, :].rearrange("i (h t) c -> i h (t c)", h=G)
                                 ).then_inc(ld_q[g], 16)
                    sp.dma_start(KL[PROD:ROWS, g, :, :], ones_l[:, hs, it * 3 * P:it * 3 * P + BW]).then_inc(ld_q[g], 16)
                    for w in range(2):
                        k0 = it * 3 * P + w * WSTEP
                        src = bass.AP(v_st.tensor, v_st.offset + k0 * NH * VC + G * g * VC,
                                      [[NH * VC, WIN], [2 * WSTEP * NH * VC, NW // 2], [1, G * VC]])
                        dst = VL[w * W:w * W + WIN, g, w:NW:2, :, :].rearrange("p w h c -> p w (h c)")
                        sp.dma_start(dst, src).then_inc(ld_q[g], 16)
            for b in range(NB):
                sp.wait_ge(y_done, NB + b + 1)
                sp.dma_start(out_t[:, b * TB:(b + 1) * TB, :], X[:, b * TB:(b + 1) * TB, :]).then_inc(x_out, 16)
            sp.wait_ge(x_out, 16 * NB)

        @block.gpsimd
        def _(pool):
            for st in range(STAGES - 2):
                pool.dma_start(WBL[:, st, :], up_w[st].rearrange("(c k) a b -> c (k a b)", c=NC)).then_inc(ld_b, 16)
            pool.dma_start(WROW2[:, :, :], up_w[STAGES - 2:STAGES].rearrange("s k a b -> s (k a b)")[None, :, :]).then_inc(ld_b, 16)
            pool.dma_start(BB[:, 0, :], b_exp.rearrange("(c p) -> c p", c=NC)).then_inc(ld_b, 16)
            pool.dma_start(UBR[:, :], up_b[None, :]).then_inc(ld_b, 16)
            pool.memset(ZR[:, :], 0.0).then_inc(zero_set, 1)
            pool.memset(ZB[:, :], 0.0).then_inc(zero_set, 1)
            pool.memset(VN[:, :, :, :], 0.0).then_inc(bias_fold, 1)
            pool.memset(VS[:, :, :, :], 0.0).then_inc(bias_fold, 1)
            pool.wait_ge(bias_fold, 2)
            pool.memset(VN[:, :, :, D:D + 1], 1.0).then_inc(zero_set, 1)
            pool.memset(VS[:, :, :, D:D + 1], 1.0).then_inc(zero_set, 1)
            k = 2

            def stage(w4, y, z, t, s, parts):
                nonlocal k
                n = y.shape[1] // (2 * s)
                yv = y.rearrange("p (n i s) -> p n i s", n=n, i=2)
                zv = z.rearrange("p (n i s) -> p n i s", n=n, i=2)
                tv = t.rearrange("p (n i s) -> p n i s", n=n, i=2)
                wv = w4.rearrange("p (n s) c -> p n c s", n=n)
                for o in range(2):
                    pool.tensor_tensor(zv[:, :, o, :], yv[:, :, o, :], wv[:, :, 3 * o, :], ALU.mult).then_inc(bias_fold, 1)
                    pool.tensor_tensor(tv[:, :, o, :], yv[:, :, 1 - o, :], wv[:, :, 1 + o, :], ALU.mult).then_inc(bias_fold, 1)
                k += 4
                pool.wait_ge(bias_fold, k)
                pool.tensor_tensor(z, z, t, ALU.add).then_inc(bias_fold, 1)
                k += 1
                pool.wait_ge(bias_fold, k)

            pool.wait_ge(ld_b, 16 * (STAGES + 1))
            a, b = 0, 1
            for st in range(STAGES - 2):
                stage(WBL[:, st, :].rearrange("p (k c) -> p k c", c=4), BB[:, a, :], BB[:, b, :], BB[:, 2, :], 2 ** st, NC)
                a, b = b, a
            for c in range(NC):
                pool.dma_start(BR[:, 0, c * P:(c + 1) * P], BB[c:c + 1, a, :]).then_inc(bias_move, 16)
            pool.wait_ge(bias_move, 16 * NC)
            a, b = 0, 1
            for st in range(STAGES - 2, STAGES):
                stage(WROW2[:, st - STAGES + 2, :].rearrange("p (k c) -> p k c", c=4), BR[:, a, :], BR[:, b, :], BR[:, 2, :], 2 ** st, 1)
                a, b = b, a
            assert a == 0
            pool.tensor_tensor(BR[:, 1, :], BR[:, 0, :], UBR[:, :], ALU.add).then_inc(bias_done, 1)

            for b in range(NB):
                f, o = b // 2, b % 2
                pool.wait_ge(qk_ready, 3 * b + 3)
                if b:
                    pool.wait_ge(nm_ps, b)
                q, ks, kl = QK[f][:, QB * o:QB * (o + 1)], QK[f][:, SOF + P * o:SOF + P * (o + 1)], \
                    QK[f][:, LOF + 3 * P * o:LOF + 3 * P * (o + 1)]
                pool.tensor_tensor(SQ[:, 0:QB], q, q, ALU.mult).then_inc(sq_done, 1)
                pool.tensor_tensor(SQ[:, QB:QB + P], ks, ks, ALU.mult).then_inc(sq_done, 1)
                pool.tensor_tensor(SQ[:, QB + P:2 * QB], kl, kl, ALU.mult).then_inc(sq_done, 1)

        @block.tensor
        def _(pe):
            pe.wait_ge(zero_set, N_MASKS)
            pe.wait_ge(one_set, 1)
            for f in range(2):
                pe.wait_ge(ld_w, 16 * (f + 1))
                for i in range(STAGES):
                    st = i if f == 0 else STAGES - 1 - i
                    n = f * STAGES + i
                    if n >= 2:
                        pe.wait_ge(fold, 5 * (n - 1) + (n - 2 >= STAGES))
                    for c in range(2):
                        o = st * 2 * HID + c * HID
                        mm = pe.matmul(PS[:, 2 * (n % 2) + c, :], ONE[:, :], WROW[:, o:o + HID], start=True, stop=True)
                    mm.then_inc(wbc, 1)
                if f == 0:
                    pe.wait_ge(ld_c, 16 * 14)
                    for c in range(NC):
                        mm = pe.transpose(PS[:, 4, c * P:(c + 1) * P], WCON[:, c, :], ID[:, :])
                    mm.then_inc(wct, 1)
            pe.wait_ge(bias_done, 1)
            for c in range(NC):
                mm = pe.matmul(PS[:, 5, c:c + 1], BR[:, 1, c * P:(c + 1) * P], ONE[:, 0:1], start=True, stop=True)
            mm.then_inc(bias_t, 1)
            pe.wait_ge(fold, FOLDS)
            for c in range(NC):
                mm = pe.transpose(PS[:, 6, c * P:(c + 1) * P], DNF[:, c * P:(c + 1) * P], ID[:, :])
            mm.then_inc(dnt, 1)

            def transpose_block(b):
                pe.wait_ge(xn_ready, b + 1)
                if b == 0:
                    pe.wait_ge(dn_done, 1)
                    pe.wait_ge(bias_move2, 1)
                else:
                    pe.wait_ge(xt_ready, b)
                for t in range(TB):
                    mm = pe.transpose(PS[:, 0, t * P:(t + 1) * P], XN[:, t, :], ID[:, :])
                mm.then_inc(xt_ps, 1)

            def ffn(b, ahead):
                pe.wait_ge(xt_ready, b + 1)
                for c in range(NC):
                    if b % NB:
                        pe.wait_ge(g_ready, NC * (b - 1) + c + 1)
                    pe.matmul(PS[:, 1 + c, :], UPW2[:, c * P:(c + 1) * P], XT[:, :], start=True, stop=True).then_inc(h_ps, 1)
                if ahead:
                    transpose_block(b + 1)
                pe.wait_ge(g_ready, NC * (b + 1))
                if b % NB:
                    pe.wait_ge(y_done, b)
                for t in range(TB):
                    for c in range(NC):
                        mm = pe.matmul(PS[:, 5, t * P:(t + 1) * P], GH[:, c, t * P:(t + 1) * P], DNW[:, c, :],
                                       start=(c == 0), stop=(c == NC - 1))
                mm.then_inc(y_ps, 1)

            transpose_block(0)
            for b in range(NB):
                ffn(b, b < NB - 1)

            def norm_sums(b):
                pe.wait_ge(sq_done, 3 * b + 3)
                if b:
                    pe.wait_ge(nm_step, b)
                for c in range(2):
                    mm = pe.matmul(PS[0:NH, 4 + c, :], HS[:, :], SQ[:, c * QB:(c + 1) * QB], start=True, stop=True)
                mm.then_inc(nm_ps, 1)

            for b in range(NB):
                pe.wait_ge(qx_ready, b + 1)
                if b == 0:
                    pe.wait_ge(y_done, NB)
                else:
                    pe.wait_ge(qt_ready, b)
                for t in range(TB):
                    mm = pe.transpose(PS[:, 0, t * P:(t + 1) * P], XN[:, t, :], ID[:, :])
                mm.then_inc(qt_ps, 1)
                pe.wait_ge(qt_ready, b + 1)
                if b:
                    pe.wait_ge(qk_ready, 3 * b)
                    pe.wait_ge(v_ready, 2 * b)
                pe.matmul(PS[:, 1, :], QW[:, :], XT[:, :], start=True, stop=True).then_inc(qkv_ps, 1)
                pe.wait_ge(qtr_ready, b + 1)
                pe.matmul(PS[:, 2, :], KW[:, :], XTR[:, :], start=True, stop=True).then_inc(qkv_ps, 1)
                for t in range(TB):
                    mm = pe.matmul(PS[:, 3, t * P:(t + 1) * P], XTR[:, t * P:(t + 1) * P], VW[:, :], start=True, stop=True)
                mm.then_inc(qkv_ps, 1)
                if b:
                    norm_sums(b - 1)
            norm_sums(NB - 1)
            pe.wait_ge(nm_step, NB + 2)
            pe.transpose(PS[0:1, 7, 0:NH], NX[:, 2:3], ID[0:NH, 0:NH]).then_inc(bt_ps, 1)

            pe.wait_ge(ld_ks, 16 * NH)
            pe.wait_ge(qk_ready, 3 * NB)
            pe.wait_ge(v_ready, 2 * NB)
            pe.wait_ge(flag_set, 1)
            with pe.If(pe.value_load(FLAG[0:1, 0:1], min_val=0, max_val=1) == 0):
                for it in range(NB):
                    pe.wait_ge(ld_mq, 16 * 2 * NH * (it + 1))
                    for t in range(TB):
                        for j in range(NG + 1):
                            n = 5 * TB * it + 5 * t + j
                            if n >= 2:
                                pe.wait_ge(mx_red, n - 1)
                            if n == 20 * it and it:
                                pe.wait_ge(mt_step, 5 * it)
                            half = 4 * (n % 2)
                            if j < NG:
                                for h in range(G):
                                    mm = pe.matmul(PS[:, half + h, :], QS[0:PROD, j, h, t * P:(t + 1) * P],
                                                   KS[0:PROD, G * j + h, :], start=True, stop=True)
                            else:
                                for c in range(2):
                                    pe.matmul(PS[:, half + c, 0:8 * WIN], IDB[:, :],
                                              MQ[:, TB * it + t:TB * it + t + 1, :].to_broadcast([P, 8, WIN]),
                                              start=True, stop=False, skip_group_check=True)
                                    for h in range(8):
                                        hh = 8 * c + h
                                        for w in range(2):
                                            q0 = t * P + w * W
                                            k0 = (2 * t + w) * WSTEP
                                            mm = pe.matmul(PS[w * W:(w + 1) * W, half + c, h * WIN:(h + 1) * WIN],
                                                           QS[0:PROD, hh // G, hh % G, q0:q0 + W],
                                                           KL[0:PROD, hh // G, hh % G, k0:k0 + WIN],
                                                           start=False, stop=(h == 7), skip_group_check=True)
                            mm.then_inc(mx_ps, 1)
                    pe.wait_ge(mx_step, 2 * (it + 1))
                    pe.transpose(PS[0:NH * TB, 0, 0:P], MX[:, :, :].rearrange("p h t -> p (h t)"), ID[:, :]).then_inc(mt_ps, 1)
                pe.wait_ge(mt_step, 5 * NB)
                pe.wait_ge(mx_red, 5 * TB * NB)
            pe.end_ifs()

            def scores(it, g, s):
                n = NSTEP * (NG * it + g) + s
                if NSTEP * g + s >= 3:
                    pe.wait_ge(p_ready, n - 2)
                b0 = 2 * (s % 3)
                if s < 8:
                    pair, h = s // G, s % G
                    for c in range(2):
                        ch = 2 * pair + c
                        mm = pe.matmul(PS[:, b0 + c, :], KS[:, G * g + h, ch * P:(ch + 1) * P], QS[:, g, h, :],
                                       start=True, stop=True)
                else:
                    for c in range(2):
                        pe.matmul(PS[:, b0 + c, :], IDB[:, :], MK[:, :], start=True, stop=False, skip_group_check=True)
                        for i in range(2):
                            h = 2 * c + i
                            for w in range(NW):
                                p0 = W * (w % 2)
                                c0 = i * QB // 2 + (w // 2) * W
                                mm = pe.matmul(PS[p0:p0 + WIN, b0 + c, c0:c0 + W],
                                               KL[:, g, h, w * WSTEP:w * WSTEP + WIN], QS[:, g, h, w * W:(w + 1) * W],
                                               start=False, stop=(w == NW - 1), skip_group_check=True)
                mm.then_inc(s_ps, 1)

            def values(it, g, pair, c):
                n = NG * it + g
                if pair == 0 and c == 0:
                    pe.wait_ge(p_ready, NSTEP * n + 4)
                    if g:
                        pe.wait_ge(o_sb, n)
                if pair == 1 and c == 0:
                    pe.wait_ge(p_ready, NSTEP * n + 8)
                for h in range(G):
                    mm = pe.matmul(PS[VC * h:VC * (h + 1), 6, :], VS[:, 2 * pair + c, G * g + h, :], PE_[:, pair, h, c, :],
                                   start=(pair == 0 and c == 0), stop=False, skip_group_check=True)
                if c == 1:
                    mm.then_inc(pv_half, 1)

            def values_local(it, g):
                n = NG * it + g
                pe.wait_ge(p_ready, NSTEP * n + 9)
                for w in range(NW):
                    for h in range(G):
                        mm = pe.matmul(PS[VC * h:VC * (h + 1), 6, w * W:(w + 1) * W], VL[:, g, w, h, :],
                                       PL[:, h, w // 2, :], start=False, stop=True, skip_group_check=True)
                mm.then_inc(o_ps, 1)

            def turn(it, g):
                n = NG * it + g
                pe.wait_ge(o_sb, n + 1)
                if n and (g or it):
                    pe.wait_ge(o_ctx, n)
                for t in range(TB):
                    mm = pe.transpose(PS[:, 7, t * P:(t + 1) * P], OS[:, t * P:(t + 1) * P], ID[:, :])
                mm.then_inc(ot_ps, 1)

            for it in range(NB):
                for g in range(NG):
                    pe.wait_ge(ld_q[g], 16 * (2 * G + 4) * (it + 1))
                    for s in range(NSTEP):
                        scores(it, g, s)
                        if g and s == 1:
                            values(it, g - 1, 1, 0)
                        if g and s == 2:
                            values(it, g - 1, 1, 1)
                        if g and s == 3:
                            values_local(it, g - 1)
                        if g and s == 5:
                            turn(it, g - 1)
                        if s == 5:
                            values(it, g, 0, 0)
                        if s == 6:
                            values(it, g, 0, 1)
                values(it, NG - 1, 1, 0)
                values(it, NG - 1, 1, 1)
                values_local(it, NG - 1)
                turn(it, NG - 1)
                pe.wait_ge(o_ctx, NG * (it + 1))
                for t in range(TB):
                    mm = pe.transpose(PS[:, 7, t * P:(t + 1) * P], CT[:, t, :], ID[:, :])
                mm.then_inc(ct_ps, 1)
                pe.wait_ge(ct_sb, it + 1)
                for t in range(TB):
                    mm = pe.matmul(PS[:, 7, t * P:(t + 1) * P], CTT[:, t * P:(t + 1) * P], OW[:, :], start=True, stop=True)
                mm.then_inc(op_ps, 1)
                pe.wait_ge(x2_done, it + 1)

            transpose_block(NB)
            for b in range(NB, 2 * NB):
                ffn(b, b < 2 * NB - 1)

        @block.scalar
        def _(act):
            act.wait_ge(ld_c, 16 * 14)
            act.activation(SG[:, 0:1], UN[:, :], ACT.Exp, scale=-1.0).then_inc(sig, 1)

            def root():
                act.activation(SD[:, :], VE[:, :], ACT.Sqrt).then_inc(ln_sd, 1)

            def ffn(b):
                act.wait_ge(xt_ps, b + 1)
                if b:
                    act.wait_ge(h_ps, NC * b)
                if b == NB:
                    act.wait_ge(qkv_ps, 3 * NB)
                act.activation(XT[:, :], PS[:, 0, :], ACT.Copy).then_inc(xt_ready, 1)
                for c in range(NC):
                    act.wait_ge(h_ps, NC * b + c + 1)
                    if b and c == 0:
                        act.wait_ge(y_ps, b)
                    if b == 0 and c == 0:
                        act.wait_ge(bias_move2, 1)
                    act.activation(GH[:, c, :], PS[:, 1 + c, :], ACT.Gelu, bias=BUP[:, c:c + 1]).then_inc(g_ready, 1)

            act.wait_ge(ln_step, LN_A)
            root()
            for b in range(NB):
                ffn(b)
            act.wait_ge(ln_step, LN_N + LN_A)
            root()
            act.wait_ge(sig, 3)
            act.wait_ge(zero_set, N_MASKS)
            for b in range(NB):
                f, o = b // 2, b % 2
                act.wait_ge(qt_ps, b + 1)
                if b:
                    act.wait_ge(qkv_ps, 3 * b)
                act.activation(XT[:, :], PS[:, 0, :], ACT.Copy).then_inc(qt_ready, 1)
                xs = PS[:, 0, :].rearrange("p (a r) -> p a r", r=STRIDE)
                act.activation(XTR[:, 0:P], xs[:, :, 0], ACT.Copy).then_inc(qtr_part, 1)
                act.activation(XTR[:, P:QB].rearrange("p (a r) -> p a r", r=STRIDE - 1), xs[:, :, 1:STRIDE],
                               ACT.Copy).then_inc(qtr_ready, 1)
                act.wait_ge(qkv_ps, 3 * b + 1)
                act.activation(QK[f][:, QB * o:QB * (o + 1)], PS[:, 1, :], ACT.Copy, scale=SG[:, 2:3]).then_inc(qk_ready, 1)
                act.wait_ge(qkv_ps, 3 * b + 2)
                act.activation(QK[f][:, SOF + P * o:SOF + P * (o + 1)], PS[:, 2, 0:P], ACT.Copy).then_inc(qk_ready, 1)
                act.activation(QK[f][:, LOF + 3 * P * o:LOF + 3 * P * (o + 1)], PS[:, 2, P:QB], ACT.Copy).then_inc(qk_ready, 1)
                act.wait_ge(qkv_ps, 3 * b + 3)
                if b:
                    act.wait_ge(v_out, 16 * b)
                act.activation(VN[:, :, :, 0:D], PS[:, 3, P:QB].rearrange("p (t h d) -> p t h d", t=3, d=D),
                               ACT.Copy).then_inc(v_ready, 1)
                act.activation(VS[:, b, :, 0:D], PS[:, 3, 0:P].rearrange("p (h d) -> p h d", d=D),
                               ACT.Copy).then_inc(v_ready, 1)

            for it in range(NB):
                for g in range(NG):
                    u = NG * it + g
                    for s in range(NSTEP):
                        n = NSTEP * u + s
                        act.wait_ge(s_ps, n + 1)
                        b0 = 2 * (s % 3)
                        if s < 8:
                            pair, h = s // G, s % G
                            if u and h == 0:
                                act.wait_ge(pv_half, 2 * (u - 1) + pair + 1)
                            act.activation(PE_[:, pair, h, :, :], PS[:, b0:b0 + 2, :], ACT.Exp).then_inc(p_ready, 1)
                        else:
                            if u:
                                act.wait_ge(o_ps, u)
                            act.activation(PL[:, :, :, :].rearrange("p h w q -> p (h w q)"),
                                           PS[:, b0:b0 + 2, :].rearrange("p a q -> p (a q)"), ACT.Exp).then_inc(p_ready, 1)

            act.wait_ge(ln_step, 2 * LN_N + LN_A)
            root()
            for b in range(NB, 2 * NB):
                ffn(b)

        @block.vector
        def _(dve):
            lnc = [0]

            def ln_link(ins):
                lnc[0] += 1
                ins.then_inc(ln_step, 1)

            def ln_stats():
                for t in range(NT):
                    ln_link(dve.bn_stats(STAT[:, t, :], X[:, t, :]))
                dve.wait_ge(ln_step, lnc[0])
                for t in range(NT):
                    ln_link(dve.bn_aggr(MV[:, t, :], STAT[:, t, :]))
                dve.wait_ge(ln_step, lnc[0])
                ln_link(dve.tensor_scalar(VE[:, :], MV[:, :, 1], EPS, None, ALU.add))
                assert lnc[0] % LN_N == LN_A

            def ln_inv(n):
                dve.wait_ge(ln_sd, n)
                ln_link(dve.reciprocal(RS[:, :], SD[:, :]))
                dve.wait_ge(ln_step, lnc[0])
                assert lnc[0] % LN_N == 0

            def normalize(b, done):
                for t in range(TB):
                    i = (b % NB) * TB + t
                    ins = dve.tensor_scalar(XN[:, t, :], X[:, i, :], MV[:, i, 0:1], RS[:, i:i + 1], ALU.subtract, ALU.mult)
                ins.then_inc(done, 1)

            def add_bias(b):
                ts = slice((b % NB) * TB, (b % NB) * TB + TB)
                dve.wait_ge(xn_ready, b + 1)
                bias = YB[:, 0:1, :].to_broadcast([P, TB, P])
                dve.scalar_tensor_tensor(X[:, ts, :], bias, 0.5, X[:, ts, :], ALU.mult, ALU.add).then_inc(r_ready, 1)

            dve.memset(ONE[:, :], 1.0).then_inc(one_set, 1)
            dve.memset(VL[:, :, :, :, :].rearrange("p g w h c -> p (g w h c)"), 0.0).then_inc(vl_zero, 1)
            dve.wait_ge(ld_x, 16)
            ln_stats()
            fc = [0]

            def fold_link(ins):
                fc[0] += 1
                ins.then_inc(fold, 1)

            def stage(n, st, y, z, t, down):
                s = 2 ** st
                m = HID // (2 * s)
                yv, zv, tv = (a.rearrange("p (n i s) -> p n i s", n=m, i=2) for a in (y, z, t))
                b0 = 2 * (n % 2)
                wv = PS[:, b0:b0 + 2, :].rearrange("p a b -> p (a b)").rearrange("p (n s c) -> p n c s", n=m, c=4)
                dve.wait_ge(wbc, n + 1)
                for o in range(2):
                    cross = (2 - o) if down else (1 + o)
                    fold_link(dve.tensor_tensor(zv[:, :, o, :], yv[:, :, o, :], wv[:, :, 3 * o, :], ALU.mult))
                    fold_link(dve.tensor_tensor(tv[:, :, o, :], yv[:, :, 1 - o, :], wv[:, :, cross, :], ALU.mult))
                dve.wait_ge(fold, fc[0])
                fold_link(dve.tensor_tensor(z, z, t, ALU.add))
                dve.wait_ge(fold, fc[0])

            dve.wait_ge(ld_e, 16)
            bufs = [UPW[:, :], UPT[:, 0, :]]
            for i in range(STAGES):
                stage(i, i, bufs[i % 2], bufs[(i + 1) % 2], UPT[:, 1, :], False)
            ln_inv(1)
            normalize(0, xn_ready)
            dve.wait_ge(wct, 1)
            fold_link(dve.tensor_copy(DNR[:, :], PS[:, 4, :]))
            dve.wait_ge(fold, fc[0])
            bufs = [DNR[:, :], UPW[:, :]]
            for i in range(STAGES):
                stage(STAGES + i, STAGES - 1 - i, bufs[i % 2], bufs[(i + 1) % 2], UPT[:, 1, :], True)
            assert fc[0] == FOLDS
            dve.wait_ge(bias_t, 1)
            dve.tensor_copy(BUP[:, :], PS[:, 5, 0:NC]).then_inc(bias_move2, 1)
            dve.wait_ge(dnt, 1)
            dve.tensor_copy(DNW[:, :, :].rearrange("p c d -> p (c d)"), PS[:, 6, :]).then_inc(dn_done, 1)
            dve.wait_ge(sig, 1)
            dve.tensor_scalar(SG[:, 1:2], SG[:, 0:1], float(np.sqrt(D)), float(np.sqrt(D)), ALU.mult, ALU.add).then_inc(sig, 1)
            dve.wait_ge(sig, 2)
            dve.reciprocal(SG[:, 2:3], SG[:, 1:2]).then_inc(sig, 1)
            dve.tensor_tensor(YB[:, 0, :], YB[:, 0, :], YB[:, 1, :], ALU.add).then_inc(r_ready, 1)
            dve.wait_ge(r_ready, 1)

            def ffn(b, ahead):
                add_bias(b)
                if ahead:
                    dve.wait_ge(xt_ps, b + 1)
                    normalize(b + 1, xn_ready)
                dve.wait_ge(r_ready, b + 2)
                dve.wait_ge(y_ps, b + 1)
                ts = slice((b % NB) * TB, (b % NB) * TB + TB)
                dve.scalar_tensor_tensor(X[:, ts, :], PS[:, 5, :].rearrange("p (t d) -> p t d", t=TB), 0.5, X[:, ts, :],
                                         ALU.mult, ALU.add).then_inc(y_done, 1)

            def split_blocks(f):
                dve.wait_ge(qk_ready, 6 * f + 6)
                if f:
                    dve.wait_ge(parts_out, 16 * 9 * f)
                dve.tensor_copy(QKP[:, 0, :], QK[f]).then_inc(split, 1)
                dve.wait_ge(split, 4 * f + 1)
                dve.tensor_tensor(QKR, QK[f], QKP[:, 0, :], ALU.subtract).then_inc(split, 1)
                dve.wait_ge(split, 4 * f + 2)
                dve.tensor_copy(QKP[:, 1, :], QKR).then_inc(split, 1)
                dve.wait_ge(split, 4 * f + 3)
                dve.tensor_tensor(QKP[:, 2, :], QKR, QKP[:, 1, :], ALU.subtract).then_inc(split, 1)

            def norms(b):
                dve.wait_ge(nm_ps, b + 1)
                dve.tensor_reduce(NM[:, b, :], PS[0:NH, 4:6, :], AX.X, ALU.max).then_inc(nm_step, 1)

            for b in range(NB):
                ffn(b, b < NB - 1)
            dve.wait_ge(y_done, NB)
            ln_stats()
            ln_inv(2)
            for b in range(NB):
                if b:
                    dve.wait_ge(qt_ps, b)
                else:
                    dve.wait_ge(xt_ps, NB)
                normalize(b, qx_ready)
                if b == 2:
                    split_blocks(0)
                if b:
                    norms(b - 1)
            split_blocks(1)
            norms(NB - 1)
            dve.wait_ge(nm_step, NB)
            dve.tensor_reduce(NX[:, 0:2], NM[:, :, :].rearrange("h b c -> h c b"), AX.X, ALU.max).then_inc(nm_step, 1)
            dve.wait_ge(nm_step, NB + 1)
            dve.tensor_tensor(NX[:, 2:3], NX[:, 0:1], NX[:, 1:2], ALU.mult).then_inc(nm_step, 1)
            dve.wait_ge(bt_ps, 1)
            dve.tensor_reduce(FLT[:, 0:1], PS[0:1, 7, 0:NH], AX.X, ALU.max).then_inc(nm_step, 1)
            dve.wait_ge(nm_step, NB + 3)
            dve.tensor_scalar(FLAG[:, :], FLT[:, 0:1], SAFE * SAFE, None, ALU.is_le).then_inc(flag_set, 1)
            dve.wait_ge(flag_set, 1)

            with dve.If(dve.value_load(FLAG[0:1, 0:1], min_val=0, max_val=1) == 0):
                for it in range(NB):
                    for t in range(TB):
                        for j in range(NG + 1):
                            n = 5 * TB * it + 5 * t + j
                            half = 4 * (n % 2)
                            dve.wait_ge(mx_ps, n + 1)
                            if j < NG:
                                dve.tensor_reduce(MXS[:, G * j:G * j + G, t], PS[:, half:half + 4, :], AX.X, ALU.max).then_inc(mx_red, 1)
                            else:
                                dve.tensor_reduce(MXL[:, :, t].rearrange("p (c h) -> p c h", c=2),
                                                  PS[:, half:half + 2, 0:8 * WIN].rearrange("p c (h k) -> p c h k", h=8),
                                                  AX.X, ALU.max).then_inc(mx_red, 1)
                    dve.wait_ge(mx_red, 5 * TB * (it + 1))
                    dve.tensor_tensor(MX[:, :, :], MXS[:, :, :], MXL[:, :, :], ALU.max).then_inc(mx_step, 1)
                    dve.wait_ge(mx_step, 2 * it + 1)
                    dve.tensor_scalar(MX[:, :, :], MX[:, :, :], -1.0, None, ALU.mult).then_inc(mx_step, 1)
                    dve.wait_ge(mt_ps, it + 1)
                    dve.tensor_copy(MT[:, :], PS[0:NH * TB, 0, 0:P]).then_inc(mt_step, 1)
                    dve.wait_ge(mt_step, 5 * it + 1)
                    if it:
                        dve.wait_ge(mx_out, 16 * it)
                    dve.tensor_copy(MP[:, 0, :], MT[:, :]).then_inc(mt_step, 1)
                    dve.wait_ge(mt_step, 5 * it + 2)
                    dve.tensor_tensor(MR[:, :], MT[:, :], MP[:, 0, :], ALU.subtract).then_inc(mt_step, 1)
                    dve.wait_ge(mt_step, 5 * it + 3)
                    dve.tensor_copy(MP[:, 1, :], MR[:, :]).then_inc(mt_step, 1)
                    dve.wait_ge(mt_step, 5 * it + 4)
                    dve.tensor_tensor(MP[:, 2, :], MR[:, :], MP[:, 1, :], ALU.subtract).then_inc(mt_step, 1)
            dve.end_ifs()

            dve.wait_ge(qx_ready, NB)
            for it in range(NB):
                ts = slice(it * TB, it * TB + TB)
                dve.tensor_tensor(X[:, ts, :], X[:, ts, :], OBB[:, None, :].to_broadcast([P, TB, P]), ALU.add).then_inc(r2_ready, 1)
                for g in range(NG):
                    n = NG * it + g
                    dve.wait_ge(o_ps, n + 1)
                    if n:
                        dve.wait_ge(ot_ps, n)
                    dve.tensor_copy(OS[:, :], PS[:, 6, :]).then_inc(o_sb, 1)
                    dve.wait_ge(ot_ps, n + 1)
                    ov = PS[:, 7, :].rearrange("p (t h c) -> p t h c", t=TB, h=G)
                    dve.reciprocal(RD[:, :, :], ov[:, :, :, D]).then_inc(o_den, 1)
                    dve.wait_ge(o_den, n + 1)
                    if g == 0 and it:
                        dve.wait_ge(ct_ps, it)
                    dve.tensor_tensor(CT[:, :, G * D * g:G * D * (g + 1)].rearrange("p t (h d) -> p t h d", h=G),
                                      ov[:, :, :, 0:D], RD[:, :, :, None].to_broadcast([P, TB, G, D]),
                                      ALU.mult).then_inc(o_ctx, 1)
                dve.wait_ge(ct_ps, it + 1)
                dve.tensor_copy(CTT[:, :], PS[:, 7, :]).then_inc(ct_sb, 1)
                dve.wait_ge(r2_ready, it + 1)
                dve.wait_ge(op_ps, it + 1)
                dve.tensor_tensor(X[:, ts, :], PS[:, 7, :].rearrange("p (t d) -> p t d", t=TB), X[:, ts, :],
                                  ALU.add).then_inc(x2_done, 1)
            dve.wait_ge(x2_done, NB)
            ln_stats()
            ln_inv(3)
            normalize(NB, xn_ready)
            for b in range(NB, 2 * NB):
                ffn(b, b < 2 * NB - 1)


def constants():
    bf = mybir.dt.np(BF16)
    n = np.arange(WIN)
    rel = STRIDE * (n // 3) + n % 3 + 1 - LOCAL
    q = np.arange(W)
    far = np.abs(rel[:, None] - q[None, :]) > LOCAL
    mk = np.full((2, W, W), BIG, np.float32)
    mk[:, :WIN, :] = np.where(far, BIG, 0.0)
    mask_k = np.tile(mk.reshape(P, W), (1, QB // W))
    mq = np.zeros((P, NT, WIN), np.float32)
    for t in range(NT):
        for w in range(2):
            key = t * P + w * W + rel
            shut = far | (key < 0)[:, None] | (key >= S)[:, None]
            mq[w * W:(w + 1) * W, t, :] = np.where(shut, BIG, 0.0).T
    ones_l = np.ones((PARTS, NH, LK), np.float32)
    ones_l[:, :, :PADK] = 0.0
    ones_l[:, :, LK - PADK:] = 0.0
    return {
        "ident": np.eye(P, dtype=np.float32), "identb": np.eye(P).astype(bf),
        "mask_k": mask_k.astype(bf), "mask_q": mq.astype(bf), "head_sel": np.kron(np.eye(NH), np.ones((D, 1))).astype(bf),
        "ones_s": np.ones((PARTS, NH, KEYS)).astype(bf), "ones_l": ones_l.astype(bf),
        "zeros_q": np.zeros((PARTS, NB, NH * TB, P)).astype(bf),
    }


_INS = ["L0_attn_x", "L0_attn_q_w", "L0_attn_k_w", "L0_attn_v_w", "L0_attn_o_w", "L0_attn_o_b", "L0_attn_unity_scale",
        "L0_ffn_W_exp", "L0_ffn_b_exp", "L0_ffn_up_weights", "L0_ffn_up_bias", "L0_ffn_down_weights", "L0_ffn_W_con",
        "L0_ffn_b_con", "L0_ffn_down_bias"]


def kernel(**inputs):
    import concourse.bacc as bacc
    from concourse.bass_utils import run_bass_kernel_spmd as run

    nc = bacc.Bacc("TRN2", target_bir_lowering=False, num_devices=1)
    arrays, args = {}, []
    for name in _INS:
        a = np.ascontiguousarray(inputs[name])
        arrays[name] = a.reshape(a.shape or (1,))
    arrays.update(constants())
    for name, a in arrays.items():
        args.append(nc.dram_tensor(name, a.shape, mybir.dt.from_np(a.dtype), kind="ExternalInput").ap())
    args.append(nc.dram_tensor("out", (1, S, P), F32, kind="ExternalOutput").ap())
    program(nc, *args)
    r = run(nc, [arrays], core_ids=[0])
    return r.results[0]["out"]
```

```python
from contextlib import ExitStack

import numpy as np

import concourse.bass as bass
from concourse import mybir

F32 = mybir.dt.float32
I32 = mybir.dt.int32
BF16 = mybir.dt.bfloat16
ACT = mybir.ActivationFunctionType
ALU = mybir.AluOpType
AX = mybir.AxisListType

P = 128
S = 2048
NT = S // P
QB = 512
NB = S // QB
TB = QB // P
HID = 512
NC = HID // P
STAGES = 9
NH = 16
D = 8
G = 4
NG = NH // G
STRIDE = 4
LOCAL = 8
KEYS = S // STRIDE
NCH = KEYS // P
PARTS = 3
PROD = PARTS * PARTS * D
ROWS = PROD + PARTS
DN_POOL = 8
WBUFS = 4
H_BANKS0 = (1, 2, 3, 0)
SLOT_LOADS = 2 * PARTS + 3
W = 64
WIN = 3 * (W + 2 * LOCAL) // 4
WSTEP = 3 * W // 4
PADK = 3 * LOCAL // 4
LK = 3 * S // 4 + 32
TK = 3 * P // 4
TWIN = TK + 2 * PADK
BW = (TB - 1) * TK + P
VC = 32
BIG = -1.0e30
EPS = 1e-5
SAFE = 40.0
SC = 2 * QB
NSTEP = 10


def program(nc, x, q_w, k_w, v_w, o_w, o_b, unity, w_exp, b_exp, up_w, up_b, dn_w, w_con, b_con, dn_b,
            ident, identb, mask_k, mask_q, head_sel, row_sel, ones_s, ones_l, zeros_q, out):
    x_t = x[0].rearrange("(t p) f -> p t f", p=P)
    out_t = out[0].rearrange("(t p) f -> p t f", p=P)

    ctx = ExitStack()
    with ctx:
        def sb(name, shape, dt=F32):
            return ctx.enter_context(nc.sbuf_tensor(name, shape, dt))

        def sem(name):
            return ctx.enter_context(nc.semaphore(name))

        q_st = nc.dram_tensor("q_parts", [NB, PARTS, P, QB], BF16, kind="Internal").ap()
        ks_st = nc.dram_tensor("k_strided_parts", [NCH, PARTS, P, P], BF16, kind="Internal").ap()
        kl_st = nc.dram_tensor("k_local_parts", [PARTS, P, LK], BF16, kind="Internal").ap()
        m_st = nc.dram_tensor("neg_max_by_query", [PARTS, NB, NH * TB, P], BF16, kind="Internal").ap()
        v_st = nc.dram_tensor("v_local_by_key", [LK, NH * VC], F32, kind="Internal").ap()

        X = sb("resid", [P, NT, P])
        N_MASKS = 2
        XN = sb("xnorm", [P, 2, TB, P])
        XT = sb("xnorm_t", [P, QB])
        GH = sb("gelu_h", [P, NC, QB])
        UPW = sb("up_folded", [P, HID])
        UPT = sb("fold_tmp", [P, 2, HID])
        DNR = sb("down_rows", [P, HID])
        DNW = sb("down_folded", [P, NC, P])
        WCON = sb("w_con_sb", [P, NC, P])
        ARENA = sb("probs_all", [P, 10 * SC])
        WROW = sb("weight_rows", [32 * PARTS, 2, HID])
        WRR = sb("weight_rest", [32 * PARTS, HID])
        WMID = sb("weight_mid", [32 * PARTS, HID], BF16)
        WPT = sb("weight_parts", [32 * PARTS, 2, HID], BF16)
        RSEL = sb("row_sel_sb", [32 * PARTS, 2 * STAGES], BF16)
        WBL = GH[0:NC, 0:4, :].rearrange("p c q -> p (c q)")[:, 0:(STAGES - 2) * HID // 2].rearrange(
            "p (s k) -> p s k", s=STAGES - 2)
        BB = sb("bias_blocks", [NC, 3, P])
        BR = sb("bias_row", [1, 3, HID])
        UBR = sb("up_bias_row", [1, HID])
        BUP = sb("bias_up", [P, NC])
        ONE = sb("ones", [1, P])
        YB = sb("ffn_bias", [P, 2, P])
        OBB = sb("o_bias", [P, P])
        STAT = sb("stats", [P, NT, 6])
        MV = sb("mean_var", [P, NT, 2])
        VE = sb("var_eps", [P, NT])
        RS = sb("rstd", [P, NT])
        ID = sb("ident_sb", [P, P])
        IDB = sb("identb_sb", [P, P], BF16)
        MK = sb("mask_k_sb", [P, P])
        MQ = sb("mask_q_sb", [P, NT, WIN], BF16)
        QW = sb("q_w_sb", [P, P])
        KW = sb("k_w_sb", [P, P])
        VW = sb("v_w_sb", [P, P])
        OW = sb("o_w_sb", [P, P])
        UN = sb("unity_sb", [P, 1])
        SG = sb("sigm", [P, 4])
        WROW2 = sb("weight_rows_last", [1, 2, 2 * HID])
        QK = [ARENA[:, o:o + 2 * QB] for o in (0, 2 * QB)]
        QKR = ARENA[:, 4 * QB:6 * QB]
        QKP = [ARENA[:, o:o + 3 * QB].bitcast(BF16).rearrange("p (i s) -> p i s", i=PARTS) for o in (6 * QB, 9 * QB)]
        SOF, LOF = QB, QB + P
        VN = sb("v_block", [P, 2, 3, NH, VC])
        VS = sb("v_strided", [P, NCH, NH, VC])
        ZR = sb("zeros", [LK - PADK - 3 * S // 4, NH * VC])
        ZB = sb("zerosb", [P, LK - PADK - 3 * S // 4], BF16)
        XN2 = sb("xnorm2", [P, TB, P])
        XT2 = sb("xnorm2_t", [P, QB])
        XTR = sb("xnorm2_t_by_key", [P, QB])
        RSN = sb("rstd_tmp", [P, NT])
        SQ = sb("squares", [P, 2 * QB], BF16)
        HS = sb("head_sel_sb", [P, 32], BF16)
        NM = sb("norms", [64, NB])
        NX = sb("norms_max", [64, 1])
        FLT = sb("bound_row", [1, 64])
        FLP = sb("bound_products", [1, NH + 1])
        FLAG = sb("bounded", [1, 1], mybir.dt.int32)
        KS = sb("k_strided", [ROWS, NCH, NH, P], BF16)
        QS = sb("q_slots", [ROWS, NG, G, QB], BF16)
        KL = sb("k_local", [ROWS, NG, G, BW], BF16)
        VL = sb("v_local", [P, NG, TB, G, VC])
        PE_ = ARENA[:, 0:8 * SC].rearrange("p (a h c q) -> p a h c q", a=2, h=G, c=2)
        PL = ARENA[:, 8 * SC:10 * SC].rearrange("p (h t q) -> p h t q", h=G, t=TB)
        OS = sb("o_sb", [P, QB])
        RD = sb("rden", [P, TB, G])
        CT = sb("ctx_rows", [P, TB, P])
        CTT = sb("ctx_t", [P, QB])
        MXS = sb("max_strided", [P, NH, TB])
        MXL = sb("max_local", [P, NH, TB])
        MX = sb("neg_max", [P, NH, TB])
        MT = sb("neg_max_t", [NH * TB, P])
        MR = sb("neg_max_rest", [NH * TB, P])
        MP = sb("neg_max_parts", [NH * TB, PARTS, P], BF16)
        PS = ctx.enter_context(nc.psum_tensor("ps", [P, 8, 512], F32))

        ld_x = sem("ld_x")
        ld_w = [sem(f"ld_w{f}") for f in range(2)]
        w_zero = sem("w_zero")
        w_split = sem("w_split")
        v_zero = sem("v_zero")
        v_ones = sem("v_ones")
        ld_e = sem("ld_e")
        ld_c = sem("ld_c")
        ld_b = sem("ld_b")
        zero_set = sem("zero_set")
        pads_out = sem("pads_out")
        wbc = sem("wbc")
        wbc_dn = sem("wbc_dn")
        fold = sem("fold")
        dn_w_sb = sem("dn_w_sb")
        dn_copy = sem("dn_copy")
        fold_p = sem("fold_p")
        fold_d = sem("fold_d")
        ld_wc = sem("ld_wc")
        wct = sem("wct")
        dnt = sem("dnt")
        dn_done = sem("dn_done")
        bias_fold = sem("bias_fold")
        bias_move = sem("bias_move")
        bias_t = sem("bias_t")
        bias_done = sem("bias_done")
        ln_step = sem("ln_step")
        xn_ready = sem("xn_ready")
        xt_ps = sem("xt_ps")
        xt_ready = sem("xt_ready")
        h_ps = sem("h_ps")
        g_ready = sem("g_ready")
        y_ps = sem("y_ps")
        y_done = sem("y_done")
        r_ready = sem("r_ready")
        x_out = sem("x_out")
        qx_ready = sem("qx_ready")
        qt_ps = sem("qt_ps")
        qt_ready = sem("qt_ready")
        qkv_ps = sem("qkv_ps")
        qk_ready = sem("qk_ready")
        v_ready = sem("v_ready")
        split = sem("split")
        ks_out = [sem(f"ks_out{b}") for b in range(NB)]
        kl_out = [sem(f"kl_out{b}") for b in range(NB)]
        q_out = [sem(f"q_out{b}") for b in range(NB)]
        pl_ready = sem("pl_ready")
        v_out = [sem(f"v_out{b}") for b in range(NB)]
        sig = sem("sig")
        ld_ks = [sem(f"ld_ks{b}") for b in range(NB)]
        ld_mq = sem("ld_mq")
        sq_done = sem("sq_done")
        nm_ps = sem("nm_ps")
        nm_step = sem("nm_step")
        bt_ps = sem("bt_ps")
        flag_set = sem("flag_set")
        mx_ps = sem("mx_ps")
        mx_red = sem("mx_red")
        mx_step = sem("mx_step")
        mt_ps = sem("mt_ps")
        mt_step = sem("mt_step")
        mx_out = sem("mx_out")
        ld_q = [sem(f"ld_q{g}") for g in range(NG)]
        s_ps = sem("s_ps")
        p_ready = sem("p_ready")
        pv_half = sem("pv_half")
        o_ps = sem("o_ps")
        o_sb = sem("o_sb")
        ot_ps = sem("ot_ps")
        o_den = sem("o_den")
        o_ctx = sem("o_ctx")
        ct_ps = sem("ct_ps")
        ct_sb = sem("ct_sb")
        op_ps = sem("op_ps")
        x2_done = sem("x2_done")
        one_set = sem("one_set")
        qtr_part = sem("qtr_part")
        qtr_ready = sem("qtr_ready")
        vl_zero = sem("vl_zero")
        bup_set = sem("bup_set")
        obias_added = sem("obias_added")
        UPW2 = UPT[:, 0, :]
        DNF, DNT = ARENA[:, 0:HID], ARENA[:, HID:2 * HID]
        DNB = ARENA[:, 2 * HID:2 * HID + WBUFS * 2 * HID].rearrange("p (n k) -> p n k", n=WBUFS)

        def swapped(ap):
            ps, n, (step, two), s = ap.ap
            return bass.AP(ap.tensor, ap.offset + step, [ps, n, [-step, two], s])

        def stage_operands(st, w, y, z, t, down):
            s = 2 ** st
            m = HID // (2 * s)
            yv, zv, tv = (a.rearrange("p (n i s) -> p n i s", n=m, i=2) for a in (y, z, t))
            wv = w.rearrange("p (n s c) -> p n c s", n=m, c=4)
            wc = wv[:, :, 1:3, :] if not down else swapped(wv[:, :, 1:3, :])
            return (zv, yv, wv[:, :, 0:4:3, :]), (tv, swapped(yv), wc)

        block = ctx.enter_context(nc.Block())

        @block.sync
        def _(sp):
            sp.wait_ge(w_zero, 1)
            for f, w in ((0, up_w), (1, dn_w)):
                for k in range(PARTS):
                    sp.dma_start(WROW[32 * k:32 * k + 2 * STAGES, f, :],
                                 w.rearrange("s (c k) a b -> (s c) (k a b)", c=2)).then_inc(ld_w[f], 16)
                if f == 0:
                    sp.dma_start(RSEL[:, :], row_sel).then_inc(ld_w[0], 16)
                    sp.dma_start(UPW[:, :], w_exp).then_inc(ld_e, 16)
            sp.dma_start(ID[:, :], ident).then_inc(ld_wc, 16)
            sp.dma_start(WCON[:, :, :], w_con.rearrange("(c p) d -> p c d", p=P)).then_inc(ld_wc, 16)
            sp.dma_start(X[:, :, :], x_t).then_inc(ld_x, 16)
            sp.dma_start(QW[:, :], q_w).then_inc(ld_c, 16)
            sp.dma_start(KW[:, :], k_w).then_inc(ld_c, 16)
            sp.dma_start(VW[:, :], v_w).then_inc(ld_c, 16)
            sp.dma_start(OW[:, :], o_w).then_inc(ld_c, 16)
            sp.dma_start(UN[:, :], unity[None, :].partition_broadcast(P).rearrange("p a b -> p (a b)")).then_inc(ld_c, 16)
            sp.dma_start(YB[:, 0, :], b_con.partition_broadcast(P)).then_inc(ld_c, 16)
            sp.dma_start(YB[:, 1, :], dn_b.partition_broadcast(P)).then_inc(ld_c, 16)
            sp.dma_start(OBB[:, :], o_b.partition_broadcast(P)).then_inc(ld_c, 16)
            sp.dma_start(IDB[:, :], identb).then_inc(ld_c, 16)
            sp.dma_start(MK[:, :], mask_k).then_inc(ld_c, 16)
            sp.dma_start(MQ[:, :, :], mask_q).then_inc(ld_c, 16)
            sp.dma_start(HS[:, :], head_sel).then_inc(ld_c, 16)
            sp.dma_start(m_st, zeros_q).then_inc(pads_out, 16)
            sp.dma_start(KS[PROD:ROWS, :, :, :], ones_s).then_inc(pads_out, 16)
            sp.wait_ge(bias_fold, 3 * (STAGES - 2))
            for c in range(NC):
                sp.dma_start(BR[:, 0, c * P:(c + 1) * P], BB[c:c + 1, (STAGES - 2) % 2, :]).then_inc(bias_move, 16)
            sp.wait_ge(zero_set, N_MASKS)
            for a, n in ((0, PADK), (PADK + 3 * S // 4, LK - PADK - 3 * S // 4)):
                sp.dma_start(kl_st[:, :, a:a + n].rearrange("j p k -> p j k"),
                             ZB[:, None, 0:n].to_broadcast([P, PARTS, n])).then_inc(pads_out, 16)
                sp.dma_start(v_st[a:a + n, :], ZR[0:n, :]).then_inc(pads_out, 16)
            sp.wait_ge(pads_out, 16 * 6)

            def load_strided(b):
                sp.wait_ge(ks_out[b], 16)
                src = bass.AP(ks_st.tensor, ks_st.offset + b * PARTS * P * P,
                              [[0, PARTS], [NH * P, PARTS * D], [1, NH * P]])
                sp.dma_start(KS[0:PROD, b, :, :].rearrange("r h k -> r (h k)"), src).then_inc(ld_ks[b], 16)

            def load_q(it, g, done):
                for i in range(PARTS):
                    src = bass.AP(q_st.tensor, q_st.offset + (it * PARTS + i) * P * QB + G * g * QB,
                                  [[0, PARTS], [NH * QB, D], [1, G * QB]])
                    rows = slice(i * PARTS * D, (i + 1) * PARTS * D)
                    sp.dma_start(QS[rows, g, :, :].rearrange("r h s -> r (h s)"), src).then_inc(done, 16)

            def load_k(it, g, done):
                keys = kl_st.rearrange("j (d h) s -> (j d) h s", h=NH)[:, G * g:G * (g + 1), it * 3 * P:it * 3 * P + BW]
                for i in range(PARTS):
                    sp.dma_start(KL[i * PARTS * D:(i + 1) * PARTS * D, g, :, :], keys).then_inc(done, 16)

            def load_max(it, g, done):
                sp.dma_start(QS[PROD:ROWS, g, :, :],
                             m_st[:, it, G * g * TB:(G * g + G) * TB, :].rearrange("i (h t) c -> i h (t c)", h=G)
                             ).then_inc(done, 16)

            def load_ones(it, g):
                hs = slice(G * g, G * g + G)
                sp.dma_start(KL[PROD:ROWS, g, :, :], ones_l[:, hs, it * 3 * P:it * 3 * P + BW]).then_inc(ld_q[g], 16)

            def load_v(it, g):
                src = bass.AP(v_st.tensor, v_st.offset + it * 3 * P * NH * VC + G * g * VC,
                              [[NH * VC, TWIN], [TK * NH * VC, TB], [1, G * VC]])
                sp.dma_start(VL[0:TWIN, g, :, :, :].rearrange("p t h c -> p t (h c)"), src).then_inc(ld_q[g], 16)

            for b in range(NB):
                sp.wait_ge(split, 4 * b + 4)
                sp.dma_start(ks_st[b].rearrange("j p k -> p j k"), QKP[b % 2][:, :, SOF:LOF]).then_inc(ks_out[b], 16)
                sp.dma_start(kl_st[:, :, PADK + 3 * P * b:PADK + 3 * P * (b + 1)].rearrange("j p k -> p j k"),
                             QKP[b % 2][:, :, LOF:2 * QB]).then_inc(kl_out[b], 16)
                sp.dma_start(q_st[b].rearrange("i p s -> p i s"), QKP[b % 2][:, :, 0:QB]).then_inc(q_out[b], 16)
                if b == 0:
                    for g in range(NG):
                        load_max(0, g, ld_q[g])
                        load_ones(0, g)
                if b == 1:
                    load_strided(0)
                    sp.wait_ge(q_out[0], 16)
                    for g in range(NG):
                        load_q(0, g, ld_q[g])
                if b == 2:
                    load_strided(1)
                    for c in range(2):
                        sp.wait_ge(kl_out[c], 16)
                        sp.wait_ge(v_out[c], 16)
                    sp.wait_ge(vl_zero, 1)
                    for g in range(NG // 2):
                        load_k(0, g, ld_q[g])
                        load_v(0, g)
            load_strided(2)
            load_strided(3)
            for g in range(NG // 2, NG):
                load_k(0, g, ld_q[g])
                load_v(0, g)

            sp.wait_ge(flag_set, 1)
            with sp.If(sp.value_load(FLAG[0:1, 0:1], min_val=0, max_val=1) == 0):
                for g in range(NG):
                    sp.wait_ge(ld_q[g], 16 * SLOT_LOADS)
                for b in range(NB):
                    sp.wait_ge(kl_out[b], 16)
                for b in range(NB):
                    sp.wait_ge(q_out[b], 16)
                for it in range(NB):
                    if it:
                        sp.wait_ge(mx_ps, 5 * TB * it)
                    for g in range(NG):
                        load_q(it, g, ld_mq)
                        load_k(it, g, ld_mq)
                    sp.wait_ge(mt_step, 5 * it + 5)
                    sp.dma_start(m_st[:, it].rearrange("i r c -> r i c"), MP[:, :, :]).then_inc(mx_out, 16)
                sp.wait_ge(mx_out, 16 * NB)
                sp.wait_ge(mx_ps, 5 * TB * NB)
                for g in range(NG):
                    load_q(0, g, ld_mq)
                    load_k(0, g, ld_mq)
                    load_max(0, g, ld_mq)
            sp.end_ifs()
            for b in range(NB):
                sp.wait_ge(kl_out[b], 16)
            for b in range(NB):
                sp.wait_ge(q_out[b], 16)
            for b in range(NB):
                sp.wait_ge(v_out[b], 16)

            for it in range(1, NB):
                for g in range(NG):
                    sp.wait_ge(o_ps, NG * (it - 1) + g + 1)
                    load_q(it, g, ld_q[g])
                    load_k(it, g, ld_q[g])
                    load_max(it, g, ld_q[g])
                    load_ones(it, g)
                    load_v(it, g)
            for b in range(NB):
                sp.wait_ge(y_done, NB + b + 1)
                sp.dma_start(out_t[:, b * TB:(b + 1) * TB, :], X[:, b * TB:(b + 1) * TB, :]).then_inc(x_out, 16)
            sp.wait_ge(x_out, 16 * NB)

        @block.gpsimd
        def _(pool):
            for st in range(STAGES - 2):
                pool.dma_start(WBL[:, st, :], up_w[st].rearrange("(c k) a b -> c (k a b)", c=NC)).then_inc(ld_b, 16)
            pool.dma_start(WROW2[:, :, :], up_w[STAGES - 2:STAGES].rearrange("s k a b -> s (k a b)")[None, :, :]).then_inc(ld_b, 16)
            pool.dma_start(BB[:, 0, :], b_exp.rearrange("(c p) -> c p", c=NC)).then_inc(ld_b, 16)
            pool.dma_start(UBR[:, :], up_b[None, :]).then_inc(ld_b, 16)
            pool.wait_ge(dn_copy, 1)
            bufs = [DNR[:, :], DNF]
            for i in range(DN_POOL):
                z, t = bufs[(i + 1) % 2], DNT
                first, second = stage_operands(STAGES - 1 - i, DNB[:, i % WBUFS], bufs[i % 2], z, t, True)
                pool.wait_ge(dn_w_sb, i + 1)
                pool.tensor_tensor(*first, ALU.mult).then_inc(fold_p, 1)
                pool.tensor_tensor(*second, ALU.mult).then_inc(fold_p, 1)
                pool.wait_ge(fold_p, 3 * i + 2)
                pool.tensor_tensor(z, z, t, ALU.add).then_inc(fold_p, 1)
                pool.wait_ge(fold_p, 3 * i + 3)
            pool.memset(ZR[:, :], 0.0).then_inc(zero_set, 1)
            pool.memset(ZB[:, :], 0.0).then_inc(zero_set, 1)
            pool.memset(VL[:, :, :, :, :].rearrange("p g w h c -> p (g w h c)"), 0.0).then_inc(vl_zero, 1)

            pool.memset(VN[:, :, :, :, :], 0.0).then_inc(v_zero, 1)
            pool.memset(VS[:, :, :, :], 0.0).then_inc(v_zero, 1)
            pool.wait_ge(v_zero, 2)
            pool.memset(VN[:, :, :, :, D:D + 1], 1.0).then_inc(v_ones, 1)
            pool.memset(VS[:, :, :, D:D + 1], 1.0).then_inc(v_ones, 1)

            for b in range(NB):
                pool.wait_ge(qk_ready, 3 * b + 3)
                if b:
                    pool.wait_ge(nm_ps, b)
                pool.tensor_tensor(SQ[:, :], QK[b % 2], QK[b % 2], ALU.mult).then_inc(sq_done, 1)

        @block.tensor
        def _(pe):
            pe.wait_ge(one_set, 1)

            def transpose_block(b):
                pe.wait_ge(xn_ready, b + 1)
                if b == 0:
                    pe.wait_ge(fold, 3 * STAGES)
                else:
                    pe.wait_ge(xt_ready, b)
                for t in range(TB):
                    mm = pe.transpose(PS[:, 0, t * P:(t + 1) * P], XN[:, b % 2, t, :], ID[:, :])
                mm.then_inc(xt_ps, 1)

            def ffn_up(b, chunks=range(NC)):
                pe.wait_ge(xt_ready, b + 1)
                if 2 <= b < NB:
                    pe.wait_ge(qk_ready, 3 * (b - 1))
                    pe.wait_ge(v_ready, 2 * (b - 1))
                for c in chunks:
                    if b % NB:
                        pe.wait_ge(g_ready, NC * (b - 1) + c + 1)
                    pe.matmul(PS[:, H_BANKS0[c] if b == 0 else 1 + c, :], UPW2[:, c * P:(c + 1) * P], XT[:, :], start=True, stop=True).then_inc(h_ps, 1)

            def broadcast(f, i):
                st = i if f == 0 else STAGES - 1 - i
                if i == 0:
                    pe.wait_ge(w_split, 5 * (f + 1))
                if f == 0 and i >= 2:
                    pe.wait_ge(fold, 3 * (i - 1))
                if f == 1 and i >= 2:
                    pe.wait_ge(dn_w_sb, i - 1)
                if f == 1 and i == 0:
                    pe.wait_ge(dn_copy, 1)
                for c in range(2):
                    r = 2 * st + c
                    mm = pe.matmul(PS[:, 4 * f + 2 * (i % 2) + c, :], RSEL[:, r:r + 1].to_broadcast([32 * PARTS, P]),
                                   WPT[:, f, :], start=True, stop=True)
                mm.then_inc(wbc_dn if f else wbc, 1)

            assert DN_POOL >= STAGES - 1
            broadcast(0, 0)
            broadcast(0, 1)
            pe.wait_ge(ld_wc, 32)
            for c in range(NC):
                mm = pe.transpose(PS[:, 4, c * P:(c + 1) * P], WCON[:, c, :], ID[:, :])
            mm.then_inc(wct, 1)
            broadcast(1, 0)
            broadcast(1, 1)
            for k in range(3):
                broadcast(0, 2 + 2 * k)
                broadcast(0, 3 + 2 * k)
                broadcast(1, 2 + k)
            broadcast(0, STAGES - 1)
            broadcast(1, 5)
            broadcast(1, 6)
            broadcast(1, 7)
            broadcast(1, 8)
            transpose_block(0)
            ffn_up(0, (0, 1, 2))
            pe.wait_ge(bias_done, 1)
            for c in range(NC):
                mm = pe.matmul(PS[:, 0, c:c + 1], BR[:, 1, c * P:(c + 1) * P], ONE[:, 0:1], start=True, stop=True)
            mm.then_inc(bias_t, 1)
            pe.wait_ge(fold_d, 3 * (STAGES - DN_POOL))
            for c in range(NC):
                mm = pe.transpose(PS[:, 6, c * P:(c + 1) * P], DNF[:, c * P:(c + 1) * P], ID[:, :])
            mm.then_inc(dnt, 1)
            pe.wait_ge(bup_set, 1)
            ffn_up(0, (3,))

            def ffn_down(b):
                if b == 0:
                    pe.wait_ge(dn_done, 1)
                pe.wait_ge(g_ready, NC * (b + 1))
                if b % NB:
                    pe.wait_ge(y_done, b)
                for t in range(TB):
                    for c in range(NC):
                        mm = pe.matmul(PS[:, 5, t * P:(t + 1) * P], GH[:, c, t * P:(t + 1) * P], DNW[:, c, :],
                                       start=(c == 0), stop=(c == NC - 1))
                mm.then_inc(y_ps, 1)

            def turn_rows(b):
                pe.wait_ge(qx_ready, b + 1)
                if b:
                    pe.wait_ge(qtr_ready, b)
                for t in range(TB):
                    mm = pe.transpose(PS[:, 6, t * P:(t + 1) * P], XN2[:, t, :], ID[:, :])
                mm.then_inc(qt_ps, 1)

            def qkv(b):
                pe.wait_ge(qt_ready, b + 1)
                if b:
                    pe.wait_ge(qk_ready, 3 * b)
                    pe.wait_ge(v_ready, 2 * b)
                pe.matmul(PS[:, 1, :], QW[:, :], XT2[:, :], start=True, stop=True).then_inc(qkv_ps, 1)
                pe.wait_ge(qtr_ready, b + 1)
                pe.matmul(PS[:, 2, :], KW[:, :], XTR[:, :], start=True, stop=True).then_inc(qkv_ps, 1)
                for t in range(TB):
                    mm = pe.matmul(PS[:, 3, t * P:(t + 1) * P], XTR[:, t * P:(t + 1) * P], VW[:, :], start=True, stop=True)
                mm.then_inc(qkv_ps, 1)

            def norm_sums(b):
                pe.wait_ge(sq_done, b + 1)
                if b:
                    pe.wait_ge(nm_step, b)
                for c in range(2):
                    mm = pe.matmul(PS[32 * c:32 * c + 32, 7, :], HS[:, :], SQ[:, QB * c:QB * (c + 1)], start=True, stop=True,
                                   skip_group_check=True)
                mm.then_inc(nm_ps, 1)

            for b in range(NB + 1):
                if 0 < b < NB:
                    ffn_up(b)
                    if b < NB - 1:
                        transpose_block(b + 1)
                if b >= 2:
                    norm_sums(b - 2)
                if b:
                    turn_rows(b - 1)
                if b < NB:
                    ffn_down(b)
                if b == 0:
                    transpose_block(1)
                if b:
                    qkv(b - 1)
            norm_sums(NB - 1)
            pe.wait_ge(nm_step, NB + 1)
            pe.transpose(PS[0:1, 7, 0:64], NX[:, :], ID[0:64, 0:64]).then_inc(bt_ps, 1)

            pe.wait_ge(qk_ready, 3 * NB)
            pe.wait_ge(v_ready, 2 * NB)
            pe.wait_ge(flag_set, 1)
            with pe.If(pe.value_load(FLAG[0:1, 0:1], min_val=0, max_val=1) == 0):
                for b in range(NB):
                    pe.wait_ge(ld_ks[b], 16)
                for it in range(NB):
                    pe.wait_ge(ld_mq, 16 * 2 * PARTS * NG * (it + 1))
                    for t in range(TB):
                        for j in range(NG + 1):
                            n = 5 * TB * it + 5 * t + j
                            if n >= 2:
                                pe.wait_ge(mx_red, n - 1)
                            if n == 20 * it and it:
                                pe.wait_ge(mt_step, 5 * it)
                            half = 4 * (n % 2)
                            if j < NG:
                                for h in range(G):
                                    mm = pe.matmul(PS[:, half + h, :], QS[0:PROD, j, h, t * P:(t + 1) * P],
                                                   KS[0:PROD, :, G * j + h, :], start=True, stop=True)
                            else:
                                for c in range(2):
                                    pe.matmul(PS[:, half + c, 0:8 * WIN], IDB[:, :],
                                              MQ[:, TB * it + t:TB * it + t + 1, :].to_broadcast([P, 8, WIN]),
                                              start=True, stop=False, skip_group_check=True)
                                    for h in range(8):
                                        hh = 8 * c + h
                                        for w in range(2):
                                            q0 = t * P + w * W
                                            k0 = (2 * t + w) * WSTEP
                                            mm = pe.matmul(PS[w * W:(w + 1) * W, half + c, h * WIN:(h + 1) * WIN],
                                                           QS[0:PROD, hh // G, hh % G, q0:q0 + W],
                                                           KL[0:PROD, hh // G, hh % G, k0:k0 + WIN],
                                                           start=False, stop=(h == 7), skip_group_check=True)
                            mm.then_inc(mx_ps, 1)
                    pe.wait_ge(mx_step, 2 * (it + 1))
                    pe.transpose(PS[0:NH * TB, 0, 0:P], MX[:, :, :].rearrange("p h t -> p (h t)"), ID[:, :]).then_inc(mt_ps, 1)
                pe.wait_ge(mt_step, 5 * NB)
                pe.wait_ge(mx_red, 5 * TB * NB)
                pe.wait_ge(ld_mq, 16 * (2 * PARTS * NG * NB + (2 * PARTS + 1) * NG))
            pe.end_ifs()

            def scores(it, g, s):
                k = NSTEP * g + s
                if it or k >= 3:
                    pe.wait_ge(p_ready, NSTEP * NG * it + k - 2 if k >= 3 else NSTEP * NG * it)
                b0 = 2 * (k % 3)
                if s < 8:
                    pair, h = s // G, s % G
                    for c in range(2):
                        ch = 2 * pair + c
                        mm = pe.matmul(PS[:, b0 + c, :], KS[:, ch, G * g + h, :], QS[:, g, h, :],
                                       start=True, stop=True)
                else:
                    for c in range(2):
                        h = 2 * (s - 8) + c
                        for t in range(TB):
                            mm = pe.matmul(PS[:, b0 + c, t * P:(t + 1) * P], KL[:, g, h, t * TK:t * TK + P],
                                           QS[:, g, h, t * P:(t + 1) * P], start=True, stop=True)
                mm.then_inc(s_ps, 1)

            def values(it, g, pair, c):
                n = NG * it + g
                if pair == 0 and c == 0:
                    pe.wait_ge(p_ready, NSTEP * n + 4)
                    if n:
                        pe.wait_ge(o_sb, n)
                if pair == 1 and c == 0:
                    pe.wait_ge(p_ready, NSTEP * n + 8)
                for h in range(G):
                    mm = pe.matmul(PS[VC * h:VC * (h + 1), 6, :], VS[:, 2 * pair + c, G * g + h, :], PE_[:, pair, h, c, :],
                                   start=(pair == 0 and c == 0), stop=False, skip_group_check=True)
                if c == 1:
                    mm.then_inc(pv_half, 1)

            def values_local(it, g):
                n = NG * it + g
                pe.wait_ge(pl_ready, 2 * n + 2)
                for t in range(TB):
                    for h in range(G):
                        mm = pe.matmul(PS[VC * h:VC * (h + 1), 6, t * P:(t + 1) * P], VL[:, g, t, h, :],
                                       PL[:, h, t, :], start=False, stop=True, skip_group_check=True)
                mm.then_inc(o_ps, 1)

            def turn(it, g):
                n = NG * it + g
                pe.wait_ge(o_sb, n + 1)
                if n:
                    pe.wait_ge(o_ctx, n)
                if g == 0 and it:
                    pe.wait_ge(x2_done, it)
                for t in range(TB):
                    mm = pe.transpose(PS[:, 7, t * P:(t + 1) * P], OS[:, t * P:(t + 1) * P], ID[:, :])
                mm.then_inc(ot_ps, 1)

            def ctx_turn(it):
                pe.wait_ge(o_ctx, NG * (it + 1))
                for t in range(TB):
                    mm = pe.transpose(PS[:, 7, t * P:(t + 1) * P], CT[:, t, :], ID[:, :])
                mm.then_inc(ct_ps, 1)

            def project(it):
                pe.wait_ge(ct_sb, it + 1)
                for t in range(TB):
                    mm = pe.matmul(PS[:, 7, t * P:(t + 1) * P], CTT[:, t * P:(t + 1) * P], OW[:, :], start=True, stop=True)
                mm.then_inc(op_ps, 1)

            for it in range(NB):
                for g in range(NG):
                    before = (it, g - 1) if g else (it - 1, NG - 1) if it else None
                    pe.wait_ge(ld_q[g], 16 * SLOT_LOADS * (it + 1))
                    for s in range(NSTEP):
                        if it == 0 and g == 0 and s in (0, G):
                            for c in range(2):
                                pe.wait_ge(ld_ks[2 * (s // G) + c], 16)
                        scores(it, g, s)
                        if before and s == 1:
                            values(*before, 1, 0)
                        if before and s == 2:
                            values(*before, 1, 1)
                        if before and s == 4:
                            values_local(*before)
                        if s == 6:
                            values(it, g, 0, 0)
                        if before and s == (7 if g else 5):
                            turn(*before)
                        if s == 7 and it and g == 0:
                            ctx_turn(it - 1)
                        if s == 8:
                            values(it, g, 0, 1)
                        if s == 9 and it and g == 0:
                            project(it - 1)
            values(NB - 1, NG - 1, 1, 0)
            values(NB - 1, NG - 1, 1, 1)
            values_local(NB - 1, NG - 1)
            transpose_block(NB)
            turn(NB - 1, NG - 1)
            ffn_up(NB)
            ctx_turn(NB - 1)
            project(NB - 1)

            for b in range(NB, 2 * NB):
                if b > NB:
                    ffn_up(b)
                if b < 2 * NB - 1:
                    transpose_block(b + 1)
                ffn_down(b)

        @block.scalar
        def _(act):
            for i in range(STAGES):
                act.wait_ge(wbc_dn, i + 1)
                if i >= WBUFS:
                    act.wait_ge(fold_p, 3 * (i - WBUFS + 1))
                act.activation(DNB[:, i % WBUFS], PS[:, 4 + 2 * (i % 2):6 + 2 * (i % 2), :].rearrange("p a b -> p (a b)"),
                               ACT.Copy).then_inc(dn_w_sb, 1)
            act.wait_ge(ld_c, 16 * 12)
            act.activation(SG[:, 0:1], UN[:, :], ACT.Exp, scale=-1.0).then_inc(sig, 1)

            def operand(b):
                act.wait_ge(xt_ps, b + 1)
                if b:
                    act.wait_ge(h_ps, NC * b)
                act.activation(XT[:, :], PS[:, 0, :], ACT.Copy).then_inc(xt_ready, 1)

            def gelu(b):
                for c in range(NC):
                    act.wait_ge(h_ps, NC * b + c + 1)
                    if b and c == 0:
                        act.wait_ge(y_ps, b)
                    if b == 0 and c == 0:
                        act.wait_ge(bias_t, 1)
                        act.activation(BUP[:, :], PS[:, 0, 0:NC], ACT.Copy).then_inc(bup_set, 1)
                        act.wait_ge(bup_set, 1)
                    act.activation(GH[:, c, :], PS[:, H_BANKS0[c] if b == 0 else 1 + c, :], ACT.Gelu, bias=BUP[:, c:c + 1]).then_inc(g_ready, 1)

            def qkv(b):
                q, sk, lk = QK[b % 2][:, 0:QB], QK[b % 2][:, SOF:LOF], QK[b % 2][:, LOF:2 * QB]
                act.wait_ge(qt_ps, b + 1)
                if b:
                    act.wait_ge(qkv_ps, 3 * b)
                act.activation(XT2[:, :], PS[:, 6, :], ACT.Copy).then_inc(qt_ready, 1)
                xs = PS[:, 6, :].rearrange("p (a r) -> p a r", r=STRIDE)
                act.activation(XTR[:, 0:P], xs[:, :, 0], ACT.Copy).then_inc(qtr_part, 1)
                act.activation(XTR[:, P:QB].rearrange("p (a r) -> p a r", r=STRIDE - 1), xs[:, :, 1:STRIDE],
                               ACT.Copy).then_inc(qtr_ready, 1)
                act.wait_ge(qkv_ps, 3 * b + 1)
                if b >= 2:
                    act.wait_ge(split, 4 * (b - 1))
                    act.wait_ge(sq_done, b - 1)
                act.activation(q, PS[:, 1, :], ACT.Copy, scale=SG[:, 2:3]).then_inc(qk_ready, 1)
                act.wait_ge(qkv_ps, 3 * b + 2)
                act.activation(sk, PS[:, 2, 0:P], ACT.Copy).then_inc(qk_ready, 1)
                act.activation(lk, PS[:, 2, P:QB], ACT.Copy).then_inc(qk_ready, 1)
                act.wait_ge(qkv_ps, 3 * b + 3)
                if b >= 2:
                    act.wait_ge(v_out[b - 2], 16)
                act.activation(VN[:, b % 2, :, :, 0:D], PS[:, 3, P:QB].rearrange("p (t h d) -> p t h d", t=3, d=D),
                               ACT.Copy).then_inc(v_ready, 1)
                act.activation(VS[:, b, :, 0:D], PS[:, 3, 0:P].rearrange("p (h d) -> p h d", d=D),
                               ACT.Copy).then_inc(v_ready, 1)
                act.wait_ge(v_ready, 2 * b + 1)
                act.dma_start(v_st[PADK + 3 * P * b:PADK + 3 * P * (b + 1), :].rearrange("(t p) c -> p t c", p=P),
                              VN[:, b % 2].rearrange("p t h c -> p t (h c)")).then_inc(v_out[b], 16)

            operand(0)
            act.wait_ge(sig, 3)
            act.activation(SG[:, 3:4], SG[:, 0:1], ACT.Gelu).then_inc(sig, 1)
            for b in range(NB + 1):
                if b < NB:
                    gelu(b)
                if b < NB - 1:
                    operand(b + 1)
                if b == 1:
                    act.wait_ge(v_ones, 2)
                if b >= 1:
                    qkv(b - 1)
            act.wait_ge(sig, 4)
            act.activation(SG[:, 3:4], SG[:, 0:1], ACT.Exp).then_inc(sig, 1)

            for b in range(NB):
                act.wait_ge(ks_out[b], 16)
            for b in range(NB):
                act.wait_ge(kl_out[b], 16)
            for b in range(NB):
                act.wait_ge(q_out[b], 16)
            for it in range(NB):
                for g in range(NG):
                    u = NG * it + g
                    for s in range(NSTEP):
                        k = NSTEP * g + s
                        act.wait_ge(s_ps, NSTEP * u + s + 1)
                        b0 = 2 * (k % 3)
                        if s < 8:
                            pair, h = s // G, s % G
                            if u and h == 0:
                                act.wait_ge(pv_half, 2 * (u - 1) + pair + 1)
                            act.activation(PE_[:, pair, h, :, :], PS[:, b0:b0 + 2, :], ACT.Exp).then_inc(p_ready, 1)
                        else:
                            if u:
                                act.wait_ge(o_ps, u)
                            h = 2 * (s - 8)
                            act.activation(PL[:, h:h + 2, :, :].rearrange("p h t q -> p h (t q)"),
                                           PS[:, b0:b0 + 2, :], ACT.Exp).then_inc(p_ready, 1)

            act.wait_ge(sig, 5)
            act.activation(SG[:, 3:4], SG[:, 0:1], ACT.Gelu).then_inc(sig, 1)
            operand(NB)
            for b in range(NB, 2 * NB):
                gelu(b)
                if b < 2 * NB - 1:
                    operand(b + 1)

        @block.vector
        def _(dve):
            lnc = [0]

            def ln_link(ins):
                lnc[0] += 1
                ins.then_inc(ln_step, 1)

            def ln_next(ins):
                ln_link(ins)
                dve.wait_ge(ln_step, lnc[0])

            def moments(a, n):
                for t in range(a, a + n):
                    ln_link(dve.bn_stats(STAT[:, t, :], X[:, t, :]))
                dve.wait_ge(ln_step, lnc[0])
                for t in range(a, a + n):
                    ln_link(dve.bn_aggr(MV[:, t, :], STAT[:, t, :]))
                dve.wait_ge(ln_step, lnc[0])

            def rstd(a, n):
                v, y, z = VE[:, a:a + n], RS[:, a:a + n], RSN[:, a:a + n]
                ln_next(dve.tensor_scalar(v, MV[:, a:a + n, 1], EPS, None, ALU.add))
                ln_next(dve.tensor_scalar(z.bitcast(I32), v.bitcast(I32), 1, None, ALU.logical_shift_right))
                ln_next(dve.tensor_scalar(y.bitcast(I32), z.bitcast(I32), -1.0, float(0x5F3759DF), ALU.mult, ALU.add))
                for _ in range(3):
                    ln_next(dve.scalar_tensor_tensor(z, y, -0.5, y, ALU.mult, ALU.mult))
                    ln_next(dve.tensor_tensor(z, z, v, ALU.mult))
                    ln_next(dve.scalar_tensor_tensor(y, z, 1.5, y, ALU.add, ALU.mult))

            def layernorm(a, n):
                moments(a, n)
                rstd(a, n)

            def normalize(b, xn, done):
                if done is xn_ready:
                    xn = xn[:, b % 2]
                for t in range(TB):
                    i = (b % NB) * TB + t
                    ins = dve.tensor_scalar(xn[:, t, :], X[:, i, :], MV[:, i, 0:1], RS[:, i:i + 1], ALU.subtract, ALU.mult)
                ins.then_inc(done, 1)

            def add_bias(b):
                ts = slice((b % NB) * TB, (b % NB) * TB + TB)
                dve.wait_ge(xn_ready, b + 1)
                bias = YB[:, 0:1, :].to_broadcast([P, TB, P])
                dve.scalar_tensor_tensor(X[:, ts, :], bias, 0.5, X[:, ts, :], ALU.mult, ALU.add).then_inc(r_ready, 1)

            dve.memset(WROW[:, :, :], 0.0).then_inc(w_zero, 1)
            dve.memset(ONE[:, :], 1.0).then_inc(one_set, 1)
            def split_weights(f):
                dve.wait_ge(ld_w[f], 16 * (PARTS + (f == 0)))
                dve.tensor_copy(WPT[:, f, :], WROW[:, f, :]).then_inc(w_split, 1)
                dve.wait_ge(w_split, 5 * f + 1)
                dve.tensor_tensor(WRR[:, :], WROW[:, f, :], WPT[:, f, :], ALU.subtract).then_inc(w_split, 1)
                dve.wait_ge(w_split, 5 * f + 2)
                dve.tensor_copy(WMID[:, :], WRR[:, :]).then_inc(w_split, 1)
                dve.wait_ge(w_split, 5 * f + 3)
                dve.tensor_copy(WPT[32:64, f, :], WMID[32:64, :]).then_inc(w_split, 1)
                dve.tensor_tensor(WPT[64:96, f, :], WRR[64:96, :], WMID[64:96, :], ALU.subtract).then_inc(w_split, 1)

            split_weights(0)
            split_weights(1)
            dve.wait_ge(wct, 1)
            dve.tensor_copy(DNR[:, :], PS[:, 4, :]).then_inc(dn_copy, 1)

            dve.wait_ge(ld_e, 16)
            bufs = [UPW[:, :], UPT[:, 0, :]]
            for i in range(STAGES):
                z, t = bufs[(i + 1) % 2], UPT[:, 1, :]
                first, second = stage_operands(i, PS[:, 2 * (i % 2):2 * (i % 2) + 2, :].rearrange("p a b -> p (a b)"), bufs[i % 2], z, t, False)
                dve.wait_ge(wbc, i + 1)
                dve.tensor_tensor(*first, ALU.mult).then_inc(fold, 1)
                dve.tensor_tensor(*second, ALU.mult).then_inc(fold, 1)
                dve.wait_ge(fold, 3 * i + 2)
                dve.tensor_tensor(z, z, t, ALU.add).then_inc(fold, 1)
                dve.wait_ge(fold, 3 * i + 3)

            def bias_stage(k, w4, y, z, t, s):
                n = y.shape[1] // (2 * s)
                yv, zv, tv = (a.rearrange("p (n i s) -> p n i s", n=n, i=2) for a in (y, z, t))
                wv = w4.rearrange("p (n s) c -> p n c s", n=n)
                dve.tensor_tensor(zv, yv, wv[:, :, 0:4:3, :], ALU.mult).then_inc(bias_fold, 1)
                dve.tensor_tensor(tv, swapped(yv), wv[:, :, 1:3, :], ALU.mult).then_inc(bias_fold, 1)
                dve.wait_ge(bias_fold, 3 * k + 2)
                dve.tensor_tensor(z, z, t, ALU.add).then_inc(bias_fold, 1)
                dve.wait_ge(bias_fold, 3 * k + 3)

            dve.wait_ge(ld_b, 16 * (STAGES + 1))
            for st in range(STAGES - 2):
                bias_stage(st, WBL[:, st, :].rearrange("p (k c) -> p k c", c=4), BB[:, st % 2, :], BB[:, (st + 1) % 2, :],
                           BB[:, 2, :], 2 ** st)
            dve.wait_ge(ld_x, 16)
            layernorm(0, NT)
            normalize(0, XN, xn_ready)
            dve.wait_ge(sig, 1)
            dve.tensor_scalar(SG[:, 1:2], SG[:, 0:1], float(np.sqrt(D)), float(np.sqrt(D)), ALU.mult, ALU.add).then_inc(sig, 1)
            dve.wait_ge(sig, 2)
            dve.reciprocal(SG[:, 2:3], SG[:, 1:2]).then_inc(sig, 1)
            dve.wait_ge(bias_move, 16 * NC)
            for k in range(2):
                st = STAGES - 2 + k
                bias_stage(st, WROW2[:, k, :].rearrange("p (k c) -> p k c", c=4), BR[:, k, :], BR[:, 1 - k, :], BR[:, 2, :], 2 ** st)
            dve.tensor_tensor(BR[:, 1, :], BR[:, 0, :], UBR[:, :], ALU.add).then_inc(bias_done, 1)

            bufs = [DNR[:, :], DNF]
            dve.wait_ge(fold_p, 3 * DN_POOL)
            for i in range(DN_POOL, STAGES):
                n = 3 * (i - DN_POOL)
                z, t = bufs[(i + 1) % 2], DNT
                first, second = stage_operands(STAGES - 1 - i, DNB[:, i % WBUFS], bufs[i % 2], z, t, True)
                dve.wait_ge(dn_w_sb, i + 1)
                dve.tensor_tensor(*first, ALU.mult).then_inc(fold_d, 1)
                dve.tensor_tensor(*second, ALU.mult).then_inc(fold_d, 1)
                dve.wait_ge(fold_d, n + 2)
                dve.tensor_tensor(z, z, t, ALU.add).then_inc(fold_d, 1)
                dve.wait_ge(fold_d, n + 3)
            dve.wait_ge(dnt, 1)
            dve.tensor_copy(DNW[:, :, :].rearrange("p c d -> p (c d)"), PS[:, 6, :]).then_inc(dn_done, 1)
            normalize(1, XN, xn_ready)
            dve.wait_ge(ld_c, 16 * 12)
            dve.tensor_tensor(YB[:, 0, :], YB[:, 0, :], YB[:, 1, :], ALU.add).then_inc(r_ready, 1)
            dve.wait_ge(r_ready, 1)

            def ffn_ahead(b):
                dve.wait_ge(xt_ps, b)
                normalize(b + 1, XN, xn_ready)

            def ffn_sum(b):
                add_bias(b)
                dve.wait_ge(r_ready, b + 2)
                dve.wait_ge(y_ps, b + 1)
                ts = slice((b % NB) * TB, (b % NB) * TB + TB)
                dve.scalar_tensor_tensor(X[:, ts, :], PS[:, 5, :].rearrange("p (t d) -> p t d", t=TB), 0.5, X[:, ts, :],
                                         ALU.mult, ALU.add).then_inc(y_done, 1)

            def split_block(b):
                dve.wait_ge(qk_ready, 3 * b + 3)
                if b >= 2:
                    dve.wait_ge(ks_out[b - 2], 16)
                    dve.wait_ge(kl_out[b - 2], 16)
                    dve.wait_ge(q_out[b - 2], 16)
                x, p = QK[b % 2], QKP[b % 2]
                dve.tensor_copy(p[:, 0, :], x).then_inc(split, 1)
                dve.wait_ge(split, 4 * b + 1)
                dve.tensor_tensor(QKR, x, p[:, 0, :], ALU.subtract).then_inc(split, 1)
                dve.wait_ge(split, 4 * b + 2)
                dve.tensor_copy(p[:, 1, :], QKR).then_inc(split, 1)
                dve.wait_ge(split, 4 * b + 3)
                dve.tensor_tensor(p[:, 2, :], QKR, p[:, 1, :], ALU.subtract).then_inc(split, 1)

            def norms(b):
                dve.wait_ge(nm_ps, b + 1)
                dve.tensor_reduce(NM[:, b:b + 1], PS[0:64, 7, :], AX.X, ALU.max).then_inc(nm_step, 1)

            for b in range(NB):
                ffn_sum(b)
                dve.wait_ge(y_done, b + 1)
                layernorm(b * TB, TB)
                if b:
                    dve.wait_ge(qt_ps, b)
                normalize(b, XN2, qx_ready)
                if b < NB - 2:
                    ffn_ahead(b + 1)
                if b >= 2:
                    norms(b - 2)
                if b:
                    split_block(b - 1)
            norms(NB - 2)
            split_block(NB - 1)
            norms(NB - 1)
            dve.wait_ge(nm_step, NB)
            dve.tensor_reduce(NX[:, :], NM[:, :], AX.X, ALU.max).then_inc(nm_step, 1)
            dve.wait_ge(bt_ps, 1)
            dve.tensor_copy(FLT[:, :], PS[0:1, 7, 0:64]).then_inc(nm_step, 1)
            dve.wait_ge(nm_step, NB + 2)
            dve.tensor_tensor(FLP[:, 0:NH], FLT[:, 0:NH], FLT[:, 32:32 + NH], ALU.mult).then_inc(nm_step, 1)
            dve.wait_ge(nm_step, NB + 3)
            dve.tensor_reduce(FLP[:, NH:NH + 1], FLP[:, 0:NH], AX.X, ALU.max).then_inc(nm_step, 1)
            dve.wait_ge(nm_step, NB + 4)
            dve.tensor_scalar(FLAG[:, :], FLP[:, NH:NH + 1], SAFE * SAFE, None, ALU.is_le).then_inc(flag_set, 1)
            dve.wait_ge(flag_set, 1)

            with dve.If(dve.value_load(FLAG[0:1, 0:1], min_val=0, max_val=1) == 0):
                for it in range(NB):
                    for t in range(TB):
                        for j in range(NG + 1):
                            n = 5 * TB * it + 5 * t + j
                            half = 4 * (n % 2)
                            dve.wait_ge(mx_ps, n + 1)
                            if j < NG:
                                dve.tensor_reduce(MXS[:, G * j:G * j + G, t], PS[:, half:half + 4, :], AX.X, ALU.max).then_inc(mx_red, 1)
                            else:
                                dve.tensor_reduce(MXL[:, :, t].rearrange("p (c h) -> p c h", c=2),
                                                  PS[:, half:half + 2, 0:8 * WIN].rearrange("p c (h k) -> p c h k", h=8),
                                                  AX.X, ALU.max).then_inc(mx_red, 1)
                    dve.wait_ge(mx_red, 5 * TB * (it + 1))
                    dve.tensor_tensor(MX[:, :, :], MXS[:, :, :], MXL[:, :, :], ALU.max).then_inc(mx_step, 1)
                    dve.wait_ge(mx_step, 2 * it + 1)
                    dve.tensor_scalar(MX[:, :, :], MX[:, :, :], -1.0, None, ALU.mult).then_inc(mx_step, 1)
                    dve.wait_ge(mt_ps, it + 1)
                    dve.tensor_copy(MT[:, :], PS[0:NH * TB, 0, 0:P]).then_inc(mt_step, 1)
                    dve.wait_ge(mt_step, 5 * it + 1)
                    if it:
                        dve.wait_ge(mx_out, 16 * it)
                    dve.tensor_copy(MP[:, 0, :], MT[:, :]).then_inc(mt_step, 1)
                    dve.wait_ge(mt_step, 5 * it + 2)
                    dve.tensor_tensor(MR[:, :], MT[:, :], MP[:, 0, :], ALU.subtract).then_inc(mt_step, 1)
                    dve.wait_ge(mt_step, 5 * it + 3)
                    dve.tensor_copy(MP[:, 1, :], MR[:, :]).then_inc(mt_step, 1)
                    dve.wait_ge(mt_step, 5 * it + 4)
                    dve.tensor_tensor(MP[:, 2, :], MR[:, :], MP[:, 1, :], ALU.subtract).then_inc(mt_step, 1)
            dve.end_ifs()

            dve.wait_ge(qx_ready, NB)
            def finish_unit(it, g):
                n = NG * it + g
                dve.wait_ge(o_ps, n + 1)
                if n:
                    dve.wait_ge(ot_ps, n)
                dve.tensor_copy(OS[:, :], PS[:, 6, :]).then_inc(o_sb, 1)
                dve.wait_ge(ot_ps, n + 1)
                ov = PS[:, 7, :].rearrange("p (t h c) -> p t h c", t=TB, h=G)
                dve.reciprocal(RD[:, :, :], ov[:, :, :, D]).then_inc(o_den, 1)
                dve.wait_ge(o_den, n + 1)
                if g == 0 and it:
                    dve.wait_ge(ct_ps, it)
                dve.tensor_tensor(CT[:, :, G * D * g:G * D * (g + 1)].rearrange("p t (h d) -> p t h d", h=G),
                                  ov[:, :, :, 0:D], RD[:, :, :, None].to_broadcast([P, TB, G, D]),
                                  ALU.mult).then_inc(o_ctx, 1)

            def finish_block(it):
                ts = slice(it * TB, it * TB + TB)
                dve.tensor_tensor(X[:, ts, :], X[:, ts, :], OBB[:, None, :].to_broadcast([P, TB, P]), ALU.add).then_inc(obias_added, 1)
                dve.wait_ge(ct_ps, it + 1)
                dve.tensor_copy(CTT[:, :], PS[:, 7, :]).then_inc(ct_sb, 1)
                dve.wait_ge(obias_added, it + 1)
                dve.wait_ge(op_ps, it + 1)
                dve.tensor_tensor(X[:, ts, :], PS[:, 7, :].rearrange("p (t d) -> p t d", t=TB), X[:, ts, :],
                                  ALU.add).then_inc(x2_done, 1)

            def mask_local(it, g):
                n = NG * it + g
                for c in range(2):
                    dve.wait_ge(p_ready, NSTEP * n + 9 + c)
                    pl = PL[:, 2 * c:2 * c + 2, :, :].rearrange("p h t q -> p (h t) q")
                    dve.scalar_tensor_tensor(pl, pl, 3.0e38, MK[:, None, :].to_broadcast([P, 2 * TB, P]), ALU.min,
                                             ALU.mult).then_inc(pl_ready, 1)

            for it in range(NB):
                for g in range(NG):
                    if g:
                        finish_unit(it, g - 1)
                    elif it:
                        finish_unit(it - 1, NG - 1)
                        finish_block(it - 1)
                    mask_local(it, g)
                    if it and g == 0:
                        dve.wait_ge(x2_done, it)
                        moments((it - 1) * TB, TB)
                    if it and g == 1:
                        rstd((it - 1) * TB, TB)
                    if it == 1 and g == 2:
                        normalize(NB, XN, xn_ready)
                    if it == 2 and g == 2:
                        ffn_ahead(NB)
            finish_unit(NB - 1, NG - 1)
            finish_block(NB - 1)
            dve.wait_ge(x2_done, NB)
            layernorm((NB - 1) * TB, TB)
            ffn_sum(NB)
            for b in range(NB + 1, 2 * NB):
                if b < 2 * NB - 1:
                    ffn_ahead(b)
                ffn_sum(b)


def constants():
    bf = mybir.dt.np(BF16)
    n = np.arange(WIN)
    rel = STRIDE * (n // 3) + n % 3 + 1 - LOCAL
    q = np.arange(W)
    far = np.abs(rel[:, None] - q[None, :]) > LOCAL
    keys = np.arange(P)
    relt = STRIDE * (keys // 3) + keys % 3 + 1 - LOCAL
    mask_k = np.where(np.abs(relt[:, None] - keys[None, :]) <= LOCAL, 1.0, 0.0)
    mq = np.zeros((P, NT, WIN), np.float32)
    for t in range(NT):
        for w in range(2):
            key = t * P + w * W + rel
            shut = far | (key < 0)[:, None] | (key >= S)[:, None]
            mq[w * W:(w + 1) * W, t, :] = np.where(shut, BIG, 0.0).T
    ones_l = np.ones((PARTS, NH, LK), np.float32)
    ones_l[:, :, :PADK] = 0.0
    ones_l[:, :, PADK + 3 * S // 4:] = 0.0
    return {
        "ident": np.eye(P, dtype=np.float32), "identb": np.eye(P).astype(bf),
        "mask_k": mask_k.astype(np.float32), "mask_q": mq.astype(bf), "head_sel": np.tile(np.eye(NH, 32), (D, 1)).astype(bf),
        "row_sel": np.tile(np.eye(32)[:, :2 * STAGES], (PARTS, 1)).astype(bf),
        "ones_s": np.ones((PARTS, NCH, NH, P)).astype(bf), "ones_l": ones_l.astype(bf),
        "zeros_q": np.zeros((PARTS, NB, NH * TB, P)).astype(bf),
    }


_INS = ["L0_attn_x", "L0_attn_q_w", "L0_attn_k_w", "L0_attn_v_w", "L0_attn_o_w", "L0_attn_o_b", "L0_attn_unity_scale",
        "L0_ffn_W_exp", "L0_ffn_b_exp", "L0_ffn_up_weights", "L0_ffn_up_bias", "L0_ffn_down_weights", "L0_ffn_W_con",
        "L0_ffn_b_con", "L0_ffn_down_bias"]


def kernel(**inputs):
    import concourse.bacc as bacc
    from concourse.bass_utils import run_bass_kernel_spmd as run

    nc = bacc.Bacc("TRN2", target_bir_lowering=False, num_devices=1)
    arrays, args = {}, []
    for name in _INS:
        a = np.ascontiguousarray(inputs[name])
        if name in ("L0_attn_q_w", "L0_attn_k_w"):
            a = np.ascontiguousarray(a.reshape(P, NH, D).transpose(0, 2, 1).reshape(P, P))
        arrays[name] = a.reshape(a.shape or (1,))
    arrays.update(constants())
    for name, a in arrays.items():
        args.append(nc.dram_tensor(name, a.shape, mybir.dt.from_np(a.dtype), kind="ExternalInput").ap())
    args.append(nc.dram_tensor("out", (1, S, P), F32, kind="ExternalOutput").ap())
    program(nc, *args)
    r = run(nc, [arrays], core_ids=[0])
    return r.results[0]["out"]
```
